# Optimizing a Trainium2 kernel written in Bass

```python
import numpy as np
import jax
import jax.numpy as jnp

def _softmax(x, axis=-1):
    return jax.nn.softmax(x, axis=axis)

def _gelu(x):
    return jax.nn.gelu(x, approximate=True)

def _silu(x):
    return jax.nn.silu(x)

def _sigmoid(x):
    return jax.nn.sigmoid(x)

def _layernorm(x, axis=-1, eps=1e-05):
    m = jnp.mean(x, axis=axis, keepdims=True)
    v = jnp.var(x, axis=axis, keepdims=True)
    return (x - m) / jnp.sqrt(v + eps)

def _scatter_add(tgt, idx, src, axis=0):
    return tgt.at[idx].add(src)

def _segment_sum(src, seg, n):
    return jax.ops.segment_sum(src, seg, n)
kernel_name = 'mk_gnn_resnorm_d2_gnn_r32_423d06'

def setup_inputs(seed: int=0):
    np.random.seed(seed)
    _w = jnp.asarray

    def _rec_inputs():
        import jax
        import jax.numpy as jnp
        _gk = jax.random.key(seed)
        x = -0.000202 + 1 * jax.random.normal(jax.random.fold_in(_gk, 1), (50000, 128), jnp.float32)
        src = jax.random.randint(jax.random.fold_in(_gk, 2), (50000,), 0, 50000, jnp.int32)
        dst = jnp.minimum((50000 * jax.random.uniform(jax.random.fold_in(_gk, 3), (50000,)) ** 2.0).astype(jnp.int32), 49999)
        _o = jnp.argsort(dst, stable=True)
        src = src[_o]
        dst = dst[_o]
        edge_attr_64 = 0.000189758 + 1.00013 * jax.random.normal(jax.random.fold_in(_gk, 11), (50000, 64), jnp.float32)
        return (x, src, dst, edge_attr_64)
    x, src, dst, edge_attr_64 = _rec_inputs()

    def _L0_gnn_setup():
        import jax, jax.numpy as jnp
        import numpy as np
        N_NODES = 50000
        N_EDGES = 25000
        D = 128
        DEPTH = 3
        key = jax.random.key(seed)
        k1, k2, k3, k4 = jax.random.split(key, 4)
        node_embedding = jax.random.normal(k1, (N_NODES, D), dtype=jnp.float32)
        incidence = jax.random.randint(k2, (2, N_EDGES), 0, N_NODES, dtype=jnp.int64)
        W_edge = jax.random.normal(k3, (D, D), dtype=jnp.float32) * (1.0 / np.sqrt(D))
        b_edge = jnp.zeros((D,), dtype=jnp.float32)
        W_agg = jax.random.normal(k4, (2 * D, D), dtype=jnp.float32) * (1.0 / np.sqrt(2 * D))
        b_agg = jnp.zeros((D,), dtype=jnp.float32)
        return {'node_embedding': node_embedding, 'incidence': incidence, 'W_edge': W_edge, 'b_edge': b_edge, 'W_agg': W_agg, 'b_agg': b_agg}
    _L0_gnn_all = _L0_gnn_setup()
    _L0_gnn_in = {k: v for k, v in _L0_gnn_all.items() if k in ('W_edge', 'b_edge', 'W_agg', 'b_agg')}
    del _L0_gnn_all

    def _L1_gnn_setup():
        import jax, jax.numpy as jnp
        import numpy as np
        N, E, D, H, ED = (50000, 25000, 128, 8, 64)
        C = D // H

        def _ln(x, g, b, eps=1e-05):
            m = jnp.mean(x, axis=-1, keepdims=True)
            v = jnp.var(x, axis=-1, keepdims=True)
            return (x - m) * jax.lax.rsqrt(v + eps) * g + b
        key = jax.random.key(seed)
        ks = jax.random.split(key, 16)
        p = lambda k, shape: jax.random.normal(k, shape, dtype=jnp.float32) * 0.05
        return {'x': jax.random.normal(ks[0], (N, D), dtype=jnp.float32), 'edge_index': jax.random.randint(ks[1], (2, E), 0, N, dtype=jnp.int64), 'edge_attr': jax.random.normal(ks[2], (E, ED), dtype=jnp.float32), 'Wq': p(ks[3], (D, D)), 'bq': jnp.zeros((D,), jnp.float32), 'Wk': p(ks[4], (D, D)), 'bk': jnp.zeros((D,), jnp.float32), 'Wv': p(ks[5], (D, D)), 'bv': jnp.zeros((D,), jnp.float32), 'We': p(ks[6], (ED, D)), 'Wskip': p(ks[7], (D, D)), 'bskip': jnp.zeros((D,), jnp.float32), 'g1': jnp.ones((D,), jnp.float32), 'b1': jnp.zeros((D,), jnp.float32), 'g2': jnp.ones((D,), jnp.float32), 'b2': jnp.zeros((D,), jnp.float32), 'Wf1': p(ks[8], (D, 4 * D)), 'bf1': jnp.zeros((4 * D,), jnp.float32), 'Wf2': p(ks[9], (4 * D, D)), 'bf2': jnp.zeros((D,), jnp.float32)}
    _L1_gnn_all = _L1_gnn_setup()
    _L1_gnn_in = {k: v for k, v in _L1_gnn_all.items() if k in ('Wq', 'bq', 'Wk', 'bk', 'Wv', 'bv', 'We', 'Wskip', 'bskip', 'g1', 'b1', 'g2', 'b2', 'Wf1', 'bf1', 'Wf2', 'bf2')}
    del _L1_gnn_all
    return {'x': x, 'src': src, 'dst': dst, 'edge_attr_64': edge_attr_64, 'L0_gnn_W_edge': _L0_gnn_in['W_edge'], 'L0_gnn_b_edge': _L0_gnn_in['b_edge'], 'L0_gnn_W_agg': _L0_gnn_in['W_agg'], 'L0_gnn_b_agg': _L0_gnn_in['b_agg'], 'L1_gnn_Wq': _L1_gnn_in['Wq'], 'L1_gnn_bq': _L1_gnn_in['bq'], 'L1_gnn_Wk': _L1_gnn_in['Wk'], 'L1_gnn_bk': _L1_gnn_in['bk'], 'L1_gnn_Wv': _L1_gnn_in['Wv'], 'L1_gnn_bv': _L1_gnn_in['bv'], 'L1_gnn_We': _L1_gnn_in['We'], 'L1_gnn_Wskip': _L1_gnn_in['Wskip'], 'L1_gnn_bskip': _L1_gnn_in['bskip'], 'L1_gnn_g1': _L1_gnn_in['g1'], 'L1_gnn_b1': _L1_gnn_in['b1'], 'L1_gnn_g2': _L1_gnn_in['g2'], 'L1_gnn_b2': _L1_gnn_in['b2'], 'L1_gnn_Wf1': _L1_gnn_in['Wf1'], 'L1_gnn_bf1': _L1_gnn_in['bf1'], 'L1_gnn_Wf2': _L1_gnn_in['Wf2'], 'L1_gnn_bf2': _L1_gnn_in['bf2']}

def reference(x, src, dst, edge_attr_64, L0_gnn_W_edge, L0_gnn_b_edge, L0_gnn_W_agg, L0_gnn_b_agg, L1_gnn_Wq, L1_gnn_bq, L1_gnn_Wk, L1_gnn_bk, L1_gnn_Wv, L1_gnn_bv, L1_gnn_We, L1_gnn_Wskip, L1_gnn_bskip, L1_gnn_g1, L1_gnn_b1, L1_gnn_g2, L1_gnn_b2, L1_gnn_Wf1, L1_gnn_bf1, L1_gnn_Wf2, L1_gnn_bf2):
    import jax
    import jax.numpy as jnp

    def _L0_gnn_ref(node_embedding, incidence, W_edge, b_edge, W_agg, b_agg):
        import jax, jax.numpy as jnp
        import numpy as np
        N_NODES = 50000
        N_EDGES = 25000
        D = 128
        DEPTH = 3
        src = incidence[1]
        dst = incidence[0]
        h = node_embedding
        for _ in range(DEPTH):
            msgs = jnp.take(h, src, axis=0)
            msgs = jax.nn.relu(msgs @ W_edge + b_edge)
            agg = jax.ops.segment_sum(msgs, dst, num_segments=N_NODES)
            h = jax.nn.relu(jnp.concatenate([agg, h], axis=-1) @ W_agg + b_agg)
        return h

    def _L1_gnn_ref(x, edge_index, edge_attr, Wq, bq, Wk, bk, Wv, bv, We, Wskip, bskip, g1, b1, g2, b2, Wf1, bf1, Wf2, bf2):
        import jax, jax.numpy as jnp
        import numpy as np
        N, E, D, H, ED = (50000, 25000, 128, 8, 64)
        C = D // H

        def _ln(x, g, b, eps=1e-05):
            m = jnp.mean(x, axis=-1, keepdims=True)
            v = jnp.var(x, axis=-1, keepdims=True)
            return (x - m) * jax.lax.rsqrt(v + eps) * g + b
        n = x.shape[0]
        src, dst = (edge_index[0], edge_index[1])
        q = (x @ Wq + bq).reshape(n, H, C)
        k = (x @ Wk + bk).reshape(n, H, C)
        v = (x @ Wv + bv).reshape(n, H, C)
        e = (edge_attr @ We).reshape(-1, H, C)
        k_j = k[src] + e
        v_j = v[src] + e
        logits = jnp.sum(q[dst] * k_j, axis=-1) / np.sqrt(C)
        m = jax.ops.segment_max(logits, dst, num_segments=n)
        ex = jnp.exp(logits - m[dst])
        denom = jax.ops.segment_sum(ex, dst, num_segments=n)
        alpha = ex / denom[dst]
        agg = jax.ops.segment_sum(alpha[..., None] * v_j, dst, num_segments=n)
        conv = agg.reshape(n, D) + x @ Wskip + bskip
        h = _ln(conv + x, g1, b1)
        ffn = jax.nn.gelu(h @ Wf1 + bf1, approximate=False) @ Wf2 + bf2
        return _ln(ffn + h, g2, b2)
    edge_index = jnp.stack([src, dst])
    x = _layernorm(x + _L0_gnn_ref(x, edge_index, L0_gnn_W_edge, L0_gnn_b_edge, L0_gnn_W_agg, L0_gnn_b_agg), axis=-1)
    x = _layernorm(x + _L1_gnn_ref(x, edge_index, edge_attr_64, L1_gnn_Wq, L1_gnn_bq, L1_gnn_Wk, L1_gnn_bk, L1_gnn_Wv, L1_gnn_bv, L1_gnn_We, L1_gnn_Wskip, L1_gnn_bskip, L1_gnn_g1, L1_gnn_b1, L1_gnn_g2, L1_gnn_b2, L1_gnn_Wf1, L1_gnn_bf1, L1_gnn_Wf2, L1_gnn_bf2), axis=-1)
    return x

_drawn_inputs = setup_inputs


def setup_inputs(seed=0):
    import zlib

    import numpy as np

    out = dict(_drawn_inputs(seed))
    spreads = {'L0_gnn_b_edge': (0.0, 0.1),
     'L0_gnn_b_agg': (0.0, 0.1),
     'L1_gnn_bq': (0.0, 0.8),
     'L1_gnn_bk': (0.0, 0.8),
     'L1_gnn_bv': (0.0, 0.272),
     'L1_gnn_bskip': (0.0, 0.1),
     'L1_gnn_g1': (1.0, 0.2),
     'L1_gnn_b1': (0.0, 0.1),
     'L1_gnn_g2': (1.0, 0.2),
     'L1_gnn_b2': (0.0, 0.1),
     'L1_gnn_bf1': (0.0, 0.1),
     'L1_gnn_bf2': (0.0, 0.1)}
    factors = {'L1_gnn_Wk': 2.763}
    for name, (base, spread) in spreads.items():
        noise = np.random.default_rng([zlib.crc32(name.encode()), seed]).standard_normal(out[name].shape)
        drawn = base * np.exp(spread * noise) if base else spread * noise
        out[name] = jnp.asarray(drawn.astype(out[name].dtype))
    for name, factor in factors.items():
        out[name] = (out[name] * factor).astype(out[name].dtype)
    return out
```

```python
import concourse.bass as bass
from concourse import mybir
from contextlib import ExitStack

F32 = mybir.dt.float32
BF16 = mybir.dt.bfloat16
I32 = mybir.dt.int32
ALU = mybir.AluOpType
ACT = mybir.ActivationFunctionType
AXX = mybir.AxisListType.X

P = 128
N = 50000
E = 50000
D = 128
ED = 64
H = 8
C = D // H
F = 4 * D
LAYERS = 3
T = 4
GR = T * P
NG = -(-N // GR)
NP = NG * GR
NT = NG * T
HALF = NG // 2
BEHIND = 2
LAST = (N - (NG - 1) * GR) // T
PAD_DST = 60000
FAR = 65536
BIG = 3.0e38
EPS = 1e-5
HEAD_SHIFT = (2 * GR).bit_length() - 1
assert NG % 2 == 0 and (N - (NG - 1) * GR) % T == 0 and N == E


def reached(eng, sem, count, base=0):
    if isinstance(count, int) and count <= 0:
        return
    eng.wait_ge(sem, base + count)
    if eng.engine == mybir.EngineType.SP:
        eng.nop(nofuse=True)


def halves(eng, body):
    body(0)
    body(1)
    with eng.Fori(2, HALF) as i:
        body(i)


def rows_of_group(t, g, width):
    return t[bass.ds(g * GR, GR), :].rearrange("(p k) f -> p (k f)", k=T)


class Core:

    def __init__(self, nc, ctx):
        self.nc, self.ctx = nc, ctx

        def dram(name, shape, dt):
            return nc.dram_tensor(name, shape, dt, kind="Internal").ap()

        self.h_cols = dram("h_cols", [D, NP], F32)
        self.msg_rows = dram("msg_rows", [2 * NP, D], F32)
        self.agg_rows = dram("agg_rows", [NP, D], F32)
        self.conv_rows = dram("conv_rows", [NP, D], F32)
        self.same_row = dram("same_row", [1, NP + 1], BF16)
        self.by_low = dram("by_low", [NP, 2], I32)
        self.by_src = dram("by_src", [NP, 2], I32)
        self.kv_rows = dram("kv_rows", [NP, 2 * D], F32)
        self.q_rows = dram("q_rows", [NP, D], F32)
        self.skip_rows = dram("skip_rows", [NP, D], F32)
        self.x1_rows = dram("x1_rows", [NP, D], F32)
        self.vj_rows = dram("vj_rows", [NP, D], F32)
        self.logit_cols = dram("logit_cols", [H, NP], F32)
        self.runmax_cols = dram("runmax_cols", [H, NP], F32)
        self.exp_cols = dram("exp_cols", [H, NP], F32)
        self.same = ctx.enter_context(nc.sbuf_tensor("same", [P, NP + 8], BF16))
        self.other_idx = ctx.enter_context(nc.sbuf_tensor("other_idx", [P, 2 * NT], I32))
        self.node_idx = ctx.enter_context(nc.sbuf_tensor("node_idx", [P, NT], I32))
        self.end_idx = ctx.enter_context(nc.sbuf_tensor("end_idx", [P, NT], I32))
        self.nodes_done = ctx.enter_context(nc.sbuf_tensor("nodes_done", [1, HALF + 8], I32))
        self.ident = ctx.enter_context(nc.sbuf_tensor("ident", [P, P], F32))
        self.earlier = ctx.enter_context(nc.sbuf_tensor("earlier", [P, P], BF16))
        self.not_earlier = ctx.enter_context(nc.sbuf_tensor("not_earlier", [P, P], BF16))
        self.digits = ctx.enter_context(nc.sbuf_tensor("digits", [P, LOW], BF16))
        self.bank = [ctx.enter_context(nc.psum_tensor(f"bank{b}", [P, 512], F32)) for b in range(8)]

        self.sems = []

    def sem(self, name):
        self.sems.append(self.nc.alloc_semaphore(name=name))
        return self.sems[-1]

    def end_stage(self):
        self.nc.clear_and_free_semaphores(self.sems)
        self.nc.all_engine_barrier()
        self.sems = []


FULL = E // (P * P) * P * P
NB = FULL // (P * P)
LOW, HIGH = 256, 256
assert NP <= LOW * HIGH and NB + 1 == T


def load_blocks(sp, tile, vec, count, shift, sem):
    mid = (count - FULL - shift) // P
    rest = count - FULL - shift - mid * P
    tail = "" if len(vec.shape) == 1 else " w"
    sp.dma_start(tile[:, 0:NB], vec[shift:shift + FULL].rearrange(f"(b j p){tail} -> j b p{tail}", b=NB, p=P)).then_inc(sem, 16)
    at = FULL + shift
    sp.dma_start(tile[0:mid, NB], vec[at:at + mid * P].rearrange(f"(j p){tail} -> j p{tail}", p=P)).then_inc(sem, 16)
    if rest:
        sp.dma_start(tile[mid:mid + 1, NB, 0:rest], vec[at + mid * P:count].rearrange(f"(a p){tail} -> a p{tail}", a=1)).then_inc(sem, 16)
    return 2 + bool(rest)


def make_identity(core):
    nc = core.nc
    done = core.sem("mask_step")
    with nc.Block() as block:
        @block.gpsimd
        def _(pool):
            pool.memset(core.ident[:, :], 0.0).then_inc(done, 1)
            pool.memset(core.earlier[:, :], 1.0).then_inc(done, 1)
            pool.memset(core.not_earlier[:, :], 1.0).then_inc(done, 1)
            pool.iota(core.digits[:, :], pattern=[[1, LOW]], base=0, channel_multiplier=0,
                      allow_small_or_imprecise_dtypes=True).then_inc(done, 1)
            pool.wait_ge(done, 4)
            pool.affine_select(out=core.ident[:, :], in_=core.ident[:, :], compare_op=ALU.not_equal, fill=1.0,
                               base=0, pattern=[[-1, P]], channel_multiplier=1).then_inc(done, 1)
            pool.affine_select(out=core.earlier[:, :], in_=core.earlier[:, :], compare_op=ALU.is_gt, fill=0.0,
                               base=0, pattern=[[1, P]], channel_multiplier=-1).then_inc(done, 1)
            pool.affine_select(out=core.not_earlier[:, :], in_=core.not_earlier[:, :], compare_op=ALU.is_ge, fill=0.0,
                               base=0, pattern=[[-1, P]], channel_multiplier=1).then_inc(done, 1)


def sort_by_src(core, dst, src):
    nc, bank = core.nc, core.bank
    with ExitStack() as s:
        def sb(name, shape, dt=F32):
            return s.enter_context(nc.sbuf_tensor(name, shape, dt))

        def two(name, shape, dt=F32):
            return [sb(f"{name}{k}", shape, dt) for k in range(2)]
        pair_i, digit_i = sb("so_pair_i", [P, T, P, 2], I32), two("so_digit_i", [P, T, P], I32)
        pair_f, digit_f = sb("so_pair_f", [P, 2, T, P]), two("so_digit_f", [P, T, P])
        table = two("so_digit_table", [P, NT])
        payload = sb("so_payload", [P, NT, 2], I32)
        ones_col, ones_row = sb("so_ones_col", [P, 1], BF16), sb("so_ones_row", [1, P])
        zero_row = sb("so_zero_row", [P, LOW], BF16)
        count, incl, base_row = two("so_count", [1, LOW]), two("so_incl", [1, LOW]), two("so_base", [1, LOW])
        onehot = two("so_onehot", [P, T, LOW], BF16)
        onehot_hi = two("so_onehot_hi", [P, T, LOW], BF16)
        picked = sb("so_picked", [P, LOW])
        pos_f, pos_i, pay = two("so_pos_f", [P, T]), two("so_pos_i", [P, T], I32), two("so_pay", [P, T, 2], I32)

        for turn, to in enumerate((core.by_low, core.by_src)):
            n = f"so{turn}_"
            filled, loaded, dig, flt, tr, tab = (core.sem(n + x) for x in ("filled", "loaded", "digits", "floats", "transposed", "tables"))
            with nc.Block() as block:
                @block.sync
                def _(sp):
                    if turn == 0:
                        sp.wait_ge(filled, 2)
                        load_blocks(sp, digit_i[0], src, E, 0, loaded)
                        load_blocks(sp, digit_i[1], dst, E, 0, loaded)
                    else:
                        load_blocks(sp, pair_i, core.by_low, NP, 0, loaded)

                @block.vector
                def _(dve):
                    if turn == 0:
                        nc.vector.memset(digit_i[0][:, :, :], NP - 1).then_inc(filled, 1)
                        nc.vector.memset(digit_i[1][:, :, :], 0).then_inc(filled, 1)
                        nc.vector.memset(ones_col[:, :], 1.0)
                        nc.vector.memset(ones_row[:, :], 1.0)
                        nc.vector.memset(zero_row[:, :], 0.0)
                        dve.wait_ge(loaded, 96)
                        for c in range(2):
                            nc.vector.tensor_copy(pair_i[:, :, :, c], digit_i[c][:, :, :]).then_inc(dig, 1)
                    else:
                        dve.wait_ge(loaded, 32)
                        dve.sem_inc(dig, 2)
                    dve.wait_ge(dig, 2)
                    nc.vector.tensor_scalar(digit_i[0][:, :, :], pair_i[:, :, :, 0], LOW - 1, None, ALU.bitwise_and).then_inc(dig, 1)
                    nc.vector.tensor_scalar(digit_i[1][:, :, :], pair_i[:, :, :, 0], 8, None, ALU.logical_shift_right).then_inc(dig, 1)
                    dve.wait_ge(dig, 4)
                    for c in range(2):
                        nc.vector.tensor_copy(digit_f[c][:, :, :], digit_i[c][:, :, :]).then_inc(flt, 1)
                        nc.vector.tensor_copy(pair_f[:, c, :, :], pair_i[:, :, :, c]).then_inc(flt, 1)
                    dve.wait_ge(tr, 4)
                    for c in range(2):
                        nc.vector.tensor_copy(table[c][:, :], bank[c][:, 0:NT]).then_inc(tab, 1)
                        nc.vector.tensor_copy(payload[:, :, c], bank[2 + c][:, 0:NT]).then_inc(tab, 1)

                @block.tensor
                def _(pe):
                    pe.wait_ge(flt, 4)
                    for c, tile in enumerate((digit_f[0], digit_f[1], pair_f[:, 0], pair_f[:, 1])):
                        for b in range(T):
                            last = nc.tensor.transpose(bank[c][:, b * P:(b + 1) * P], tile[:, b, :], core.ident[:, :])
                        last.then_inc(tr, 1)

            if turn == 0:
                hot, cnt, hist, scan_ok, base_ok = (core.sem(n + x) for x in ("onehots", "counted", "counts", "inclusive", "bases"))
                with nc.Block() as block:
                    @block.vector
                    def _(dve):
                        def body(i):
                            for k in range(2):
                                g = 2 * i + k
                                reached(dve, cnt, g - 1)
                                for c, hots in enumerate((onehot, onehot_hi)):
                                    for t in range(T):
                                        last = nc.vector.tensor_scalar(hots[k][:, t, :], core.digits[:, :],
                                                                       table[c][:, bass.ds(g * T + t, 1)], None, ALU.is_equal)
                                last.then_inc(hot, 1)
                        halves(dve, body)
                        dve.wait_ge(cnt, NG)
                        for c in range(2):
                            nc.vector.tensor_copy(count[c][:, :], bank[c][0:1, 0:LOW]).then_inc(hist, 1)
                        dve.wait_ge(hist, 2)
                        for c in range(2):
                            nc.vector.tensor_tensor_scan(incl[c][:, :], count[c][:, :], count[c][:, :], 0.0, ALU.add, ALU.bypass).then_inc(scan_ok, 1)
                        dve.wait_ge(scan_ok, 2)
                        for c in range(2):
                            nc.vector.tensor_tensor(base_row[c][:, :], incl[c][:, :], count[c][:, :], ALU.subtract).then_inc(base_ok, 1)

                    @block.tensor
                    def _(pe):
                        for c in range(2):
                            nc.tensor.matmul(bank[c][0:1, 0:LOW], ones_col[:, :], zero_row[:, :], start=True, stop=True)

                        def body(i):
                            for k in range(2):
                                pe.wait_ge(hot, 2 * i + k + 1)
                                pe.nop(nofuse=True)
                                for t in range(T):
                                    for c, hots in enumerate((onehot, onehot_hi)):
                                        last = nc.tensor.matmul(bank[c][0:1, 0:LOW], ones_col[:, :], hots[k][:, t, :],
                                                                start=False, stop=True, skip_group_check=True)
                                last.then_inc(cnt, 1)
                        halves(pe, body)

            hot, v_ok, v_read, pos_ok, int_ok, pay_ok = (core.sem(n + x) for x in (
                "rank_onehots", "ranks_ready", "ranks_read", "positions", "position_ints", "payload_ready"))
            moved = [core.sem(f"{n}moved{k}") for k in range(2)]
            V = bank[4][:, 0:LOW]
            with nc.Block() as block:
                @block.vector
                def _(dve):
                    def onehots(g, k):
                        reached(dve, v_ok, T * (g - 1) + 1)
                        for t in range(T):
                            last = nc.vector.tensor_scalar(onehot[k][:, t, :], core.digits[:, :],
                                                           table[turn][:, bass.ds(g * T + t, 1)], None, ALU.is_equal)
                        last.then_inc(hot, 1)

                    def pick(g, k, i):
                        for t in range(T):
                            dve.wait_ge(v_ok, T * g + t + 1)
                            if t == 0:
                                reached(dve, int_ok, g - 1)
                            reached(dve, v_read, T * g + t)
                            nc.vector.tensor_tensor_reduce(out=picked[:, :], in0=onehot[k][:, t, :], in1=V, scale=1.0, scalar=0.0,
                                                           op0=ALU.mult, op1=ALU.add, accum_out=pos_f[k][:, t:t + 1]).then_inc(v_read, 1)
                        dve.wait_ge(v_read, T * g + T)
                        reached(dve, moved[k], 64 * i)
                        nc.vector.tensor_copy(pos_i[k][:, :], pos_f[k][:, :]).then_inc(int_ok, 1)

                    def body(i):
                        for k in range(2):
                            g = 2 * i + k
                            onehots(g, k)
                            if k == 1:
                                pick(2 * i, 0, i)
                            elif not (isinstance(i, int) and i == 0):
                                pick(2 * i - 1, 1, i - 1)
                    halves(dve, body)
                    pick(NG - 1, 1, HALF - 1)

                @block.tensor
                def _(pe):
                    nc.tensor.matmul(V, ones_row[:, :], base_row[turn][:, :], start=True, stop=True)

                    def body(i):
                        for k in range(2):
                            g = 2 * i + k
                            pe.wait_ge(hot, g + 1)
                            pe.nop(nofuse=True)
                            for t in range(T):
                                first = isinstance(g, int) and g == 0 and t == 0
                                reached(pe, v_read, T * g + t)
                                if not first:
                                    before = onehot[k][:, t - 1, :] if t else onehot[1 - k][:, T - 1, :]
                                    nc.tensor.matmul(V, core.not_earlier[:, :], before, start=False, stop=True, skip_group_check=True)
                                nc.tensor.matmul(V, core.earlier[:, :], onehot[k][:, t, :], start=False, stop=True,
                                                 skip_group_check=True).then_inc(v_ok, 1)
                    halves(pe, body)

                @block.scalar
                def _(act):
                    def body(i):
                        for k in range(2):
                            reached(act, moved[k], 64 * i)
                            nc.scalar.activation(pay[k][:, :, :], payload[:, bass.ds((2 * i + k) * T, T), :], ACT.Copy).then_inc(pay_ok, 1)
                    halves(act, body)

                @block.gpsimd
                def _(pool):
                    def body(i):
                        for k in range(2):
                            pool.wait_ge(pay_ok, 2 * i + k + 1)
                            pool.wait_ge(int_ok, 2 * i + k + 1)
                            pool.nop(nofuse=True)
                            for t in range(T):
                                pool.indirect_dma_start(to, bass.IndirectOffsetOnAxis(ap=pos_i[k][:, t:t + 1], axis=0),
                                                        pay[k][:, t, :], None, bounds_check=NP - 1, oob_is_err=False).then_inc(moved[k], 16)
                    halves(pool, body)
                    for k in range(2):
                        pool.wait_ge(moved[k], 64 * HALF)


def index_tables(core, name, load, paired, clear, first_nodes=None):
    nc = core.nc
    ZC = 14
    with ExitStack() as s:
        def sb(nm, shape, dt):
            return s.enter_context(nc.sbuf_tensor(name + nm, shape, dt))
        wide = [P, T, P, 2] if paired else [P, T, P]
        here_t, after_t = sb("here_i", wide, I32), sb("after_i", wide, I32)
        other_t = None if paired else sb("other_i", wide, I32)
        here_i, after_i = ((t[:, :, :, 0] if paired else t[:, :, :]) for t in (here_t, after_t))
        other_i = here_t[:, :, :, 1] if paired else other_t[:, :, :]
        here_f, after_f, other_f = (sb(x, [P, T, P], F32) for x in ("here_f", "after_f", "other_f"))
        eq_f, end_f, cap_f = (sb(x, [P, T, P], F32) for x in ("eq_f", "end_f", "cap_f"))
        eq_b = sb("eq_b", [P, T, P], BF16)
        tabs_sb = (core.other_idx, core.node_idx, core.end_idx)
        heads = sb("heads", [1, HALF], I32)
        first0 = sb("first0", [1, 1], BF16)
        zeros = sb("zeros", [P, NP * D // (ZC * P)], F32)
        filled, loaded, float_ok, eq_ok, stored, tabs, transposed, same_ok, heads_in = (core.sem(name + x) for x in (
            "filled", "loaded", "floats", "equal", "stored", "tables", "transposed", "flags", "heads_in"))
        block = s.enter_context(nc.Block())
        count = []

        @block.sync
        def _(sp):
            sp.wait_ge(filled, 5)
            count.append(16 * load(sp, here_t, after_t, other_t, loaded))
            if first_nodes is not None:
                with nc.allow_non_contiguous_dma(reason="one number of every 2 GR edges"):
                    sp.dma_start(heads[:, :], first_nodes).then_inc(heads_in, 16)
            out = 0
            for rows in clear:
                parts = rows.rearrange("(c p r) f -> c p (r f)", c=ZC, p=P)
                for c in range(ZC):
                    sp.dma_start(parts[c], zeros[:, :]).then_inc(stored, 16)
                out += ZC
            sp.wait_ge(eq_ok, 3)
            sp.dma_start(core.same_row[0:1, 0:1], first0[:, :]).then_inc(same_ok, 16)
            sp.dma_start(core.same_row[0:1, 1:1 + NB * P * P].rearrange("a (b j p) -> (a j) b p", b=NB, p=P),
                         eq_b[:, 0:NB, :]).then_inc(same_ok, 16)
            sp.dma_start(core.same_row[0:1, 1 + NB * P * P:1 + NP].rearrange("a (j p) -> (a j) p", p=P),
                         eq_b[0:NT - NB * P, NB, :]).then_inc(same_ok, 16)
            sp.wait_ge(same_ok, 48)
            sp.dma_start(core.same[:, 0:NP], core.same_row[0, 0:NP].partition_broadcast(P)).then_inc(stored, 16)
            sp.wait_ge(stored, 16 * (out + 1))

        @block.vector
        def _(dve):
            nc.vector.memset(here_i, PAD_DST).then_inc(filled, 1)
            nc.vector.memset(other_i, 0).then_inc(filled, 1)
            nc.vector.memset(after_t[:, :, :, :] if paired else after_i, PAD_DST + 1).then_inc(filled, 1)
            nc.vector.memset(first0[:, :], 0.0).then_inc(filled, 1)
            nc.vector.memset(zeros[:, :], 0.0)
            nc.vector.memset(core.same[:, NP:NP + 8], 0.0).then_inc(filled, 1)
            dve.wait_ge(loaded, count[0])
            nc.vector.tensor_copy(here_f[:, :, :], here_i).then_inc(float_ok, 1)
            nc.vector.tensor_copy(after_f[:, :, :], after_i).then_inc(float_ok, 1)
            nc.vector.tensor_copy(other_f[:, :, :], other_i).then_inc(float_ok, 1)
            dve.wait_ge(float_ok, 3)
            nc.vector.tensor_tensor(eq_f[:, :, :], here_f[:, :, :], after_f[:, :, :], ALU.is_equal).then_inc(eq_ok, 1)
            nc.vector.tensor_scalar(cap_f[:, :, :], here_f[:, :, :], float(N - 1), None, ALU.min).then_inc(eq_ok, 1)
            dve.wait_ge(eq_ok, 2)
            nc.vector.tensor_copy(eq_b[:, :, :], eq_f[:, :, :]).then_inc(eq_ok, 1)
            nc.vector.scalar_tensor_tensor(out=end_f[:, :, :], in0=eq_f[:, :, :], scalar=float(FAR), in1=here_f[:, :, :],
                                           op0=ALU.mult, op1=ALU.add).then_inc(eq_ok, 1)
            for n in range(3):
                dve.wait_ge(transposed, n + 1)
                nc.vector.tensor_copy(tabs_sb[n][:, 0:NT], core.bank[n][:, 0:NT]).then_inc(tabs, 1)
            nc.vector.tensor_scalar(core.other_idx[:, NT:2 * NT], core.bank[0][:, 0:NT], float(NP), None, ALU.add).then_inc(tabs, 1)
            if first_nodes is not None:
                nc.vector.memset(core.nodes_done[:, :], 0).then_inc(tabs, 1)
                dve.wait_ge(heads_in, 16)
                dve.wait_ge(tabs, 5)
                nc.vector.tensor_scalar(core.nodes_done[0:1, BEHIND + 1:HALF + 1], heads[0:1, 1:HALF + 1 - BEHIND], HEAD_SHIFT, None,
                                        ALU.logical_shift_right).then_inc(tabs, 1)

        @block.tensor
        def _(pe):
            pe.wait_ge(float_ok, 3)
            for n, (tile, ready) in enumerate(((other_f, 2), (cap_f, 3), (end_f, 4))):
                pe.wait_ge(eq_ok, ready)
                for b in range(T):
                    last = nc.tensor.transpose(core.bank[n][:, b * P:(b + 1) * P], tile[:, b, :], core.ident[:, :])
                last.then_inc(transposed, 1)


def message_passing(core, x, W_edge, b_edge, W_agg, b_agg):
    nc, bank, ident = core.nc, core.bank, core.ident
    with ExitStack() as s:
        def sb(name, shape, dt=F32):
            return s.enter_context(nc.sbuf_tensor(name, shape, dt))

        def two(name, shape, dt=F32):
            return [sb(f"{name}{k}", shape, dt) for k in range(2)]
        w_edge, w_agg_a, w_agg_h = sb("mp_w_edge", [D, D]), sb("mp_w_agg_a", [D, D]), sb("mp_w_agg_h", [D, D])
        bias_edge, bias_agg = sb("mp_b_edge", [D, 1]), sb("mp_b_agg", [D, 1])
        rows_in = two("mp_rows_in", [P, GR])
        h_in, h_out = two("mp_h_in", [D, GR]), two("mp_h_out", [D, GR])
        msg_out = two("mp_msg_out", [P, GR])
        src_ix, end_ix = two("mp_src_ix", [P, T], I32), two("mp_end_ix", [P, T], I32)
        gathered = two("mp_gathered", [P, T, D])
        relu_msg, run_sum = two("mp_relu_msg", [D, GR]), two("mp_run_sum", [D, GR])
        seg_rows = two("mp_seg_rows", [P, T, D])
        wts = core.sem("mp_weights_in")
        x_in, x_t = [core.sem(f"mp_x_in{k}") for k in range(2)], core.sem("mp_x_transposed")

        h0_ok, m0_mm, m0_ok = core.sem("mp_h0_ready"), core.sem("mp_m0_product"), core.sem("mp_m0_ready")
        h0_st, m0_st = [core.sem(f"mp_h0_stored{k}") for k in range(2)], [core.sem(f"mp_m0_stored{k}") for k in range(2)]
        with nc.Block() as block:
            @block.sync
            def _(sp):
                with nc.allow_non_contiguous_dma(reason="one bias value per partition"):
                    sp.dma_start(w_edge[:, :], W_edge).then_inc(wts, 16)
                    sp.dma_start(w_agg_a[:, :], W_agg[0:D, :]).then_inc(wts, 16)
                    sp.dma_start(w_agg_h[:, :], W_agg[D:2 * D, :]).then_inc(wts, 16)
                    sp.dma_start(bias_edge[:, :], b_edge.rearrange("(p a) -> p a", a=1)).then_inc(wts, 16)
                    sp.dma_start(bias_agg[:, :], b_agg.rearrange("(p a) -> p a", a=1)).then_inc(wts, 16)

                def load(g, k, i):
                    reached(sp, x_t, g - 1)
                    if isinstance(g, int) and g == NG - 1:
                        sp.dma_start(rows_in[k][0:LAST, :], x[g * GR:N, :].rearrange("(p k) f -> p (k f)", k=T)).then_inc(x_in[k], 16)
                    else:
                        sp.dma_start(rows_in[k][:, :], rows_of_group(x, g, D)).then_inc(x_in[k], 16)

                def store(g, k):
                    reached(sp, h0_ok, g + 1)
                    sp.dma_start(core.h_cols[:, bass.ds(g * GR, GR)], h_out[k][:, :]).then_inc(h0_st[k], 16)
                    reached(sp, m0_ok, g + 1)
                    sp.dma_start(rows_of_group(core.msg_rows, g, D), msg_out[k][:, :]).then_inc(m0_st[k], 16)

                def body(i):
                    for k in range(2):
                        load(2 * i + k, k, i)
                    for k in range(2):
                        if not (isinstance(i, int) and i == 0):
                            store(2 * i - 2 + k, k)
                body(0)
                body(1)
                with sp.Fori(2, HALF - 1) as i:
                    body(i)
                body(HALF - 1)
                for k in range(2):
                    store(NG - 2 + k, k)
                for k in range(2):
                    sp.wait_ge(h0_st[k], 16 * HALF)
                    sp.wait_ge(m0_st[k], 16 * HALF)

            @block.tensor
            def _(pe):
                pe.wait_ge(wts, 5 * 16)

                def turn(g, k, i):
                    pe.wait_ge(x_in[k], 16 * (i + 1))
                    reached(pe, h0_ok, g - 1)
                    for t in range(T):
                        last = nc.tensor.transpose(bank[k][:, t * P:(t + 1) * P], rows_in[k][:, t * D:(t + 1) * D], ident[:, :])
                    last.then_inc(x_t, 1)

                def messages(g, k):
                    pe.wait_ge(h0_ok, g + 1)
                    reached(pe, m0_ok, g - 1)
                    for t in range(T):
                        last = nc.tensor.matmul(bank[2 + k][:, t * P:(t + 1) * P], h_out[k][:, t * P:(t + 1) * P], w_edge[:, :],
                                                start=True, stop=True)
                    last.then_inc(m0_mm, 1)

                def body(i):
                    for k in range(2):
                        turn(2 * i + k, k, i)
                        if not (isinstance(i, int) and i == 0 and k == 0):
                            messages(2 * i + k - 1, 1 - k)
                halves(pe, body)
                messages(NG - 1, 1)

            @block.scalar
            def _(act):
                def body(i):
                    for k in range(2):
                        g = 2 * i + k
                        act.wait_ge(x_t, g + 1)
                        reached(act, h0_st[k], 16 * i)
                        reached(act, m0_mm, g - 1)
                        nc.scalar.activation(h_out[k][:, :], bank[k][:, :], ACT.Copy).then_inc(h0_ok, 1)
                halves(act, body)

            @block.vector
            def _(dve):
                def body(i):
                    for k in range(2):
                        g = 2 * i + k
                        dve.wait_ge(m0_mm, g + 1)
                        reached(dve, m0_st[k], 16 * i)
                        nc.vector.tensor_copy(msg_out[k][:, :], bank[2 + k][:, :]).then_inc(m0_ok, 1)
                halves(dve, body)

            @block.gpsimd
            def _(pool):
                pool.wait_ge(wts, 5 * 16)

        g_in = [core.sem(f"mp_gathered{k}") for k in range(2)]
        sc_out = [core.sem(f"mp_scattered{k}") for k in range(2)]
        ix_ok = core.sem("mp_index_ready")
        g_t, relu_ok, sum_ok = core.sem("mp_gather_transposed"), core.sem("mp_relu_ready"), core.sem("mp_sum_ready")
        seg_mm, seg_ok = core.sem("mp_segment_product"), core.sem("mp_segment_rows_ready")
        nd_in = [core.sem(f"mp_node_in{k}") for k in range(2)]
        h_mm, h_ok, m_mm, m_ok = (core.sem(n) for n in ("mp_h_product", "mp_h_ready", "mp_m_product", "mp_m_ready"))
        h_st, m_st = [core.sem(f"mp_h_stored{k}") for k in range(2)], [core.sem(f"mp_m_stored{k}") for k in range(2)]

        def layer_work(eng, edge, node):
            edge(0)
            edge(1)
            with eng.Fori(2, HALF) as i:
                edge(i)
                done = eng.value_load(core.nodes_done[0:1, bass.ds(i, 1)], min_val=0, max_val=HALF - 1)
                due = eng.value_load(core.nodes_done[0:1, bass.ds(i + 1, 1)], min_val=0, max_val=HALF - 1)
                with eng.If(done < due):
                    with eng.Fori(done, due) as n:
                        node(n, i + 1 - BEHIND)
            done = eng.value_load(core.nodes_done[0:1, HALF:HALF + 1], min_val=0, max_val=HALF - 1)
            with eng.Fori(done, HALF) as n:
                node(n, HALF)

        with nc.Block() as block:
            @block.sync
            def _(sp):
                with sp.Fori(0, LAYERS) as layer:
                    base, turn = layer * NG, layer * HALF

                    def node(n, summed):
                        for k in range(2):
                            reached(sp, sc_out[k], 64 * summed, turn * 64)
                        for k in range(2):
                            g = 2 * n + k
                            sp.dma_start(rows_in[k][:, :], rows_of_group(core.agg_rows, g, D)).then_inc(nd_in[k], 16)
                            sp.dma_start(h_in[k][:, :], core.h_cols[:, bass.ds(g * GR, GR)]).then_inc(nd_in[k], 16)
                        for k in range(2):
                            g = 2 * n + k
                            reached(sp, h_ok, g + 1, base)
                            sp.dma_start(core.h_cols[:, bass.ds(g * GR, GR)], h_out[k][:, :]).then_inc(h_st[k], 16)
                        for k in range(2):
                            g = 2 * n + k
                            to = ((layer + 1) & 1) * NP + g * GR
                            reached(sp, m_ok, g + 1, base)
                            sp.dma_start(core.msg_rows[bass.ds(to, GR), :].rearrange("(p k) f -> p (k f)", k=T),
                                         msg_out[k][:, :]).then_inc(m_st[k], 16)
                        for k in range(2):
                            reached(sp, h_st[k], 16 * (n + 1), turn * 16)
                            reached(sp, m_st[k], 16 * (n + 1), turn * 16)
                    layer_work(sp, lambda i: None, node)

            @block.gpsimd
            def _(pool):
                with pool.Fori(0, LAYERS) as layer:
                    base, turn = layer * NG, layer * HALF

                    def gather(i, k):
                        reached(pool, g_in[k], 64 * i, turn * 64)
                        reached(pool, g_t, 2 * i + k - 1, base)
                        pool.nop(nofuse=True)
                        at = (layer & 1) * NT + (2 * i + k) * T
                        nc.gpsimd.tensor_copy(src_ix[k][:, :], core.other_idx[:, bass.ds(at, T)]).then_inc(ix_ok, 1)

                    def gather_start(i, k, step):
                        pool.wait_ge(ix_ok, 2 * base + 4 * i + step)
                        pool.nop(nofuse=True)
                        for t in range(T):
                            pool.indirect_dma_start(gathered[k][:, t, :], None, core.msg_rows,
                                                    bass.IndirectOffsetOnAxis(ap=src_ix[k][:, t:t + 1], axis=0)).then_inc(g_in[k], 16)

                    def scatter(i, k, j, step):
                        reached(pool, sc_out[k], 64 * i, turn * 64)
                        pool.nop(nofuse=True)
                        nc.gpsimd.tensor_copy(end_ix[k][:, :], core.end_idx[:, bass.ds((2 * i + k) * T, T)]).then_inc(ix_ok, 1)
                        pool.wait_ge(ix_ok, 2 * base + 4 * j + step)
                        pool.wait_ge(seg_ok, base + 2 * i + k + 1)
                        pool.nop(nofuse=True)
                        for t in range(T):
                            pool.indirect_dma_start(core.agg_rows, bass.IndirectOffsetOnAxis(ap=end_ix[k][:, t:t + 1], axis=0),
                                                    seg_rows[k][:, t, :], None, bounds_check=NP - 1, oob_is_err=False).then_inc(sc_out[k], 16)

                    def body(i):
                        for k in range(2):
                            if isinstance(i, int) and i == 0:
                                gather(0, k)
                                gather_start(0, k, k + 1)
                            else:
                                gather(i, k)
                                gather_start(i, k, 2 * k - 1)
                                scatter(i - 1, k, i, 2 * k)
                    halves(pool, body)
                    for k in range(2):
                        scatter(HALF - 1, k, HALF, k - 1)
                    for k in range(2):
                        pool.wait_ge(m_st[k], turn * 16 + 16 * HALF)
                    pool.nop(nofuse=True)

            @block.tensor
            def _(pe):
                with pe.Fori(0, LAYERS) as layer:
                    base, turn = layer * NG, layer * HALF

                    def edge(i):
                        for k in range(2):
                            g = 2 * i + k
                            pe.wait_ge(g_in[k], turn * 64 + 64 * (i + 1))
                            reached(pe, relu_ok, g - 1, base)
                            for t in range(T):
                                last = nc.tensor.transpose(bank[k][:, t * P:(t + 1) * P], gathered[k][:, t, :], ident[:, :])
                            last.then_inc(g_t, 1)
                            pe.wait_ge(sum_ok, base + g + 1)
                            reached(pe, seg_ok, g - 1, base)
                            for t in range(T):
                                last = nc.tensor.matmul(bank[2 + k][:, t * P:(t + 1) * P], run_sum[k][:, t * P:(t + 1) * P],
                                                        w_agg_a[:, :], start=True, stop=True)
                            last.then_inc(seg_mm, 1)

                    def node(n, summed):
                        for k in range(2):
                            pe.wait_ge(nd_in[k], turn * 32 + 32 * (n + 1))
                            for t in range(T):
                                part = slice(t * P, (t + 1) * P)
                                nc.tensor.matmul(bank[4 + k][:, part], w_agg_h[:, :], h_in[k][:, part], start=True, stop=False)
                                last = nc.tensor.matmul(bank[4 + k][:, part], rows_in[k][:, part], ident[:, :], start=False, stop=True)
                            last.then_inc(h_mm, 1)
                        for k in range(2):
                            pe.wait_ge(h_ok, base + 2 * n + k + 1)
                            for t in range(T):
                                last = nc.tensor.matmul(bank[6 + k][:, t * P:(t + 1) * P], h_out[k][:, t * P:(t + 1) * P], w_edge[:, :],
                                                        start=True, stop=True)
                            last.then_inc(m_mm, 1)
                    layer_work(pe, edge, node)

            @block.scalar
            def _(act):
                with act.Fori(0, LAYERS) as layer:
                    base, turn = layer * NG, layer * HALF

                    def edge(i):
                        for k in range(2):
                            g = 2 * i + k
                            act.wait_ge(g_t, base + g + 1)
                            reached(act, sum_ok, g - 1, base)
                            nc.scalar.activation(relu_msg[k][:, :], bank[k][:, :], ACT.Relu, bias=bias_edge[:, 0:1]).then_inc(relu_ok, 1)
                            act.wait_ge(seg_mm, base + g + 1)
                            reached(act, sc_out[k], 64 * i, turn * 64)
                            nc.scalar.activation(seg_rows[k][:, :, :], bank[2 + k][:, :], ACT.Copy).then_inc(seg_ok, 1)

                    def node(n, summed):
                        for k in range(2):
                            act.wait_ge(h_mm, base + 2 * n + k + 1)
                            nc.scalar.activation(h_out[k][:, :], bank[4 + k][:, :], ACT.Relu, bias=bias_agg[:, 0:1]).then_inc(h_ok, 1)
                    layer_work(act, edge, node)

            @block.vector
            def _(dve):
                with dve.Fori(0, LAYERS) as layer:
                    base, turn = layer * NG, layer * HALF

                    def edge(i):
                        for k in range(2):
                            g = 2 * i + k
                            start = 0.0 if isinstance(g, int) and g == 0 else run_sum[1 - k][:, GR - 1:GR]
                            dve.wait_ge(relu_ok, base + g + 1)
                            reached(dve, seg_mm, g - 1, base)
                            reached(dve, sum_ok, g, base)
                            nc.vector.tensor_tensor_scan(run_sum[k][:, :], core.same[:, bass.ds(g * GR, GR)], relu_msg[k][:, :],
                                                         start, ALU.mult, ALU.add).then_inc(sum_ok, 1)

                    def node(n, summed):
                        for k in range(2):
                            dve.wait_ge(m_mm, base + 2 * n + k + 1)
                            nc.vector.tensor_copy(msg_out[k][:, :], bank[6 + k][:, :]).then_inc(m_ok, 1)
                    layer_work(dve, edge, node)


def norm_stats(nc, dve, chain, at, rows, stats, moments):
    for t in range(T):
        last = nc.vector.bn_stats(stats[:, t, :], rows[:, t, :])
    last.then_inc(chain, 1)
    dve.wait_ge(chain, at + 1)
    dve.nop(nofuse=True)
    for t in range(T):
        last = nc.vector.bn_aggr(moments[:, t, :], stats[:, t, :])
    return last


def inverse_deviation(nc, pool, chain, at, moments, eps_var, half, out):
    pool.nop(nofuse=True)
    nc.gpsimd.tensor_scalar(eps_var[:, :], moments[:, :, 1], EPS, None, ALU.add).then_inc(chain, 1)
    pool.wait_ge(chain, at + 1)
    return nc.gpsimd.tensor_tensor(out[:, :], eps_var[:, :], half[:, :], ALU.pow)


def project_nodes(core, x, w, b):
    nc, bank, ident = core.nc, core.bank, core.ident
    NPJ = 4 * D
    with ExitStack() as s:
        def sb(name, shape, dt=F32):
            return s.enter_context(nc.sbuf_tensor(name, shape, dt))

        def two(name, shape, dt=F32):
            return [sb(f"{name}{k}", shape, dt) for k in range(2)]
        weights, bias = sb("pn_weights", [D, NPJ]), sb("pn_bias", [P, NPJ])
        x_in, h_in = two("pn_x_in", [P, T, D]), two("pn_h_in", [D, GR])
        y = two("pn_y", [P, T, D])
        stats, moments = two("pn_stats", [P, T, 6]), two("pn_moments", [P, T, 2])
        half, eps_var, rstd = sb("pn_half", [P, T]), two("pn_eps_var", [P, T]), two("pn_rstd", [P, T])
        x1, x1_cols = two("pn_x1", [P, T, D]), two("pn_x1_cols", [D, GR])
        proj = two("pn_proj", [P, T, NPJ])
        wts, half_ok = core.sem("pn_weights_in"), core.sem("pn_half_ready")
        ld = [core.sem(f"pn_in{k}") for k in range(2)]
        h_t, y_ok, mom_ok, pow_c, rstd_ok, x1_ok = (core.sem("pn_" + n) for n in (
            "h_transposed", "dve_chain", "moments_ready", "pow_chain", "rstd_ready", "x1_ready"))
        x1_t, cols_ok, mm, pr_ok, proj_ok = (core.sem("pn_" + n) for n in (
            "x1_transposed", "x1_cols_ready", "product", "bias_added", "proj_ready"))
        st = [core.sem(f"pn_stored{k}") for k in range(2)]
        block = s.enter_context(nc.Block())

        @block.sync
        def _(sp):
            for n, name in enumerate(("Wk", "Wv", "Wq", "Wskip")):
                sp.dma_start(weights[:, n * D:(n + 1) * D], w[name]).then_inc(wts, 16)
            for n, name in enumerate(("bk", "bv", "bq", "bskip")):
                sp.dma_start(bias[:, n * D:(n + 1) * D], b[name].partition_broadcast(P)).then_inc(wts, 16)

            def load(g, k):
                reached(sp, mom_ok, g - 1)
                if isinstance(g, int) and g == NG - 1:
                    sp.dma_start(x_in[k][0:LAST, :, :], x[g * GR:N, :].rearrange("(p k) f -> p k f", k=T)).then_inc(ld[k], 16)
                else:
                    sp.dma_start(x_in[k][:, :, :], x[bass.ds(g * GR, GR), :].rearrange("(p k) f -> p k f", k=T)).then_inc(ld[k], 16)
                sp.dma_start(h_in[k][:, :], core.h_cols[:, bass.ds(g * GR, GR)]).then_inc(ld[k], 16)

            def store(g, k):
                reached(sp, proj_ok, g + 1)
                rows = lambda t: t[bass.ds(g * GR, GR), :].rearrange("(p k) f -> p k f", k=T)
                sp.dma_start(rows(core.kv_rows), proj[k][:, :, 0:2 * D]).then_inc(st[k], 16)
                sp.dma_start(rows(core.q_rows), proj[k][:, :, 2 * D:3 * D]).then_inc(st[k], 16)
                sp.dma_start(rows(core.skip_rows), proj[k][:, :, 3 * D:4 * D]).then_inc(st[k], 16)
                sp.dma_start(rows(core.x1_rows), x1[k][:, :, :]).then_inc(st[k], 16)

            def body(i):
                for k in range(2):
                    load(2 * i + k, k)
                for k in range(2):
                    if not (isinstance(i, int) and i == 0):
                        store(2 * i - 2 + k, k)
            body(0)
            body(1)
            with sp.Fori(2, HALF - 1) as i:
                body(i)
            body(HALF - 1)
            for k in range(2):
                store(NG - 2 + k, k)
            for k in range(2):
                sp.wait_ge(st[k], 64 * HALF)

        @block.tensor
        def _(pe):
            pe.wait_ge(wts, 8 * 16)

            def project(g, k):
                pe.wait_ge(x1_ok, g + 1)
                reached(pe, cols_ok, g - 1)
                for t in range(T):
                    last = nc.tensor.transpose(bank[2 + k][:, t * P:(t + 1) * P], x1[k][:, t, :], ident[:, :])
                last.then_inc(x1_t, 1)
                pe.wait_ge(cols_ok, g + 1)
                reached(pe, pr_ok, 4 * g)
                for t in range(T):
                    nc.tensor.matmul(bank[4 + t][:, :], x1_cols[k][:, t * P:(t + 1) * P], weights[:, :],
                                     start=True, stop=True).then_inc(mm, 1)

            def body(i):
                for k in range(2):
                    g = 2 * i + k
                    pe.wait_ge(ld[k], 32 * (i + 1))
                    reached(pe, mom_ok, g - 1)
                    for t in range(T):
                        last = nc.tensor.transpose(bank[k][:, t * P:(t + 1) * P], h_in[k][:, t * P:(t + 1) * P], ident[:, :])
                    last.then_inc(h_t, 1)
                    if not (isinstance(i, int) and i == 0 and k == 0):
                        project(2 * i + k - 1, 1 - k)
            halves(pe, body)
            project(NG - 1, 1)

        @block.scalar
        def _(act):
            def body(i):
                for k in range(2):
                    g = 2 * i + k
                    act.wait_ge(x1_t, g + 1)
                    reached(act, mm, 4 * (g - 1))
                    nc.scalar.activation(x1_cols[k][:, :], bank[2 + k][:, :], ACT.Copy).then_inc(cols_ok, 1)
            halves(act, body)

        @block.gpsimd
        def _(pool):
            nc.gpsimd.memset(half[:, :], -0.5).then_inc(half_ok, 1)
            pool.wait_ge(half_ok, 1)

            def body(i):
                for k in range(2):
                    g = 2 * i + k
                    pool.wait_ge(mom_ok, g + 1)
                    reached(pool, x1_ok, g - 1)
                    inverse_deviation(nc, pool, pow_c, g, moments[k], eps_var[k], half, rstd[k]).then_inc(rstd_ok, 1)
            halves(pool, body)

        @block.vector
        def _(dve):
            dve.wait_ge(wts, 8 * 16)

            def finish(g, k):
                for t in range(T):
                    dve.wait_ge(mm, 4 * g + t + 1)
                    if t == 0:
                        reached(dve, st[k], (g // 2) * 64 if isinstance(g, int) else 0)
                    nc.vector.tensor_tensor(proj[k][:, t, :], bank[4 + t][:, :], bias[:, :], ALU.add).then_inc(pr_ok, 1)
                dve.wait_ge(pr_ok, 4 * g + 4)
                nc.vector.tensor_tensor(proj[k][:, :, 3 * D:4 * D], proj[k][:, :, 3 * D:4 * D], x1[k][:, :, :], ALU.add).then_inc(proj_ok, 1)

            def body(i):
                for k in range(2):
                    g = 2 * i + k
                    dve.wait_ge(h_t, g + 1)
                    dve.wait_ge(ld[k], 32 * (i + 1))
                    reached(dve, x1_ok, g - 1)
                    nc.vector.tensor_tensor(y[k][:, :, :], bank[k][:, :].rearrange("p (t f) -> p t f", t=T), x_in[k][:, :, :], ALU.add).then_inc(y_ok, 1)
                    dve.wait_ge(y_ok, 2 * g + 1)
                    reached(dve, rstd_ok, g - 1)
                    norm_stats(nc, dve, y_ok, 2 * g + 1, y[k], stats[k], moments[k]).then_inc(mom_ok, 1)
                    dve.wait_ge(mom_ok, g + 1)
                    dve.wait_ge(rstd_ok, g + 1)
                    reached(dve, st[k], 64 * i)
                    for t in range(T):
                        last = nc.vector.tensor_scalar(x1[k][:, t, :], y[k][:, t, :], moments[k][:, t, 0:1], rstd[k][:, t:t + 1],
                                                       ALU.subtract, ALU.mult)
                    last.then_inc(x1_ok, 1)
                    if not (isinstance(i, int) and i == 0 and k == 0):
                        finish(2 * i + k - 1, 1 - k)
            halves(dve, body)
            dve.wait_ge(x1_ok, NG)
            finish(NG - 1, 1)


def edge_logits(core, edge_attr, We):
    nc, bank, ident = core.nc, core.bank, core.ident
    with ExitStack() as s:
        def sb(name, shape, dt=F32):
            return s.enter_context(nc.sbuf_tensor(name, shape, dt))

        def two(name, shape, dt=F32):
            return [sb(f"{name}{k}", shape, dt) for k in range(2)]
        w_e = sb("el_we", [ED, D])
        src_ix, dst_ix = two("el_src_ix", [P, T], I32), two("el_dst_ix", [P, T], I32)
        kv, q = two("el_kv", [P, T, 2 * D]), two("el_q", [P, T, D])
        attr, attr_cols = two("el_attr", [P, T, ED]), two("el_attr_cols", [ED, GR])
        kv_e, prod = two("el_kv_e", [P, T, 2, D]), two("el_prod", [P, T, D])
        logits = two("el_logits", [P, T, H])
        logit_c, brk, runmax = two("el_logit_c", [H, GR]), two("el_break", [H, GR]), two("el_runmax", [H, GR])
        wts, zeroed, rest_in = core.sem("el_weights_in"), core.sem("el_zeroed"), core.sem("el_rest_in")
        ix_ok = core.sem("el_index_ready")
        g_in, a_in, st_v, st_l = ([core.sem(f"el_{n}{k}") for k in range(2)] for n in (
            "gathered", "attr_in", "vj_stored", "logits_stored"))
        a_t, a_ok, e_mm, sum_ok, prod_ok, log_ok, log_t, logc_ok, brk_ok, max_ok = (core.sem("el_" + n) for n in (
            "attr_transposed", "attr_cols_ready", "e_product", "kv_e_ready", "prod_ready", "logits_ready",
            "logits_transposed", "logit_cols_ready", "break_ready", "runmax_ready"))
        block = s.enter_context(nc.Block())

        @block.sync
        def _(sp):
            sp.dma_start(w_e[:, :], We).then_inc(wts, 16)
            sp.wait_ge(zeroed, 2)

            def load(g, k, i):
                reached(sp, a_t, g - 1)
                if isinstance(g, int) and g == NG - 1:
                    whole, rest = (E - g * GR) // P, (E - g * GR) % P
                    sp.dma_start(attr[k][0:rest, whole, :], edge_attr[g * GR + whole * P:E, :]).then_inc(rest_in, 16)
                    sp.wait_ge(rest_in, 16)
                    sp.dma_start(attr[k][:, 0:whole, :], edge_attr[g * GR:g * GR + whole * P, :].rearrange("(t p) f -> p t f", p=P)).then_inc(a_in[k], 16)
                else:
                    sp.dma_start(attr[k][:, :, :], edge_attr[bass.ds(g * GR, GR), :].rearrange("(t p) f -> p t f", p=P)).then_inc(a_in[k], 16)

            def store(g, k):
                reached(sp, sum_ok, g + 1)
                sp.dma_start(core.vj_rows[bass.ds(g * GR, GR), :].rearrange("(t p) f -> p t f", p=P), kv_e[k][:, :, 1, :]).then_inc(st_v[k], 16)
                reached(sp, logc_ok, g + 1)
                sp.dma_start(core.logit_cols[:, bass.ds(g * GR, GR)], logit_c[k][:, :]).then_inc(st_l[k], 16)
                reached(sp, max_ok, g + 1)
                sp.dma_start(core.runmax_cols[:, bass.ds(g * GR, GR)], runmax[k][:, :]).then_inc(st_l[k], 16)

            def body(i):
                for k in range(2):
                    load(2 * i + k, k, i)
                    if not (isinstance(i, int) and i == 0):
                        store(2 * i - 2 + k, k)
            body(0)
            body(1)
            with sp.Fori(2, HALF - 1) as i:
                body(i)
            body(HALF - 1)
            for k in range(2):
                store(NG - 2 + k, k)
            for k in range(2):
                sp.wait_ge(st_v[k], 16 * HALF)
                sp.wait_ge(st_l[k], 32 * HALF)

        @block.gpsimd
        def _(pool):
            def body(i):
                for k in range(2):
                    g = 2 * i + k
                    reached(pool, prod_ok, g - 1)
                    pool.nop(nofuse=True)
                    nc.gpsimd.tensor_copy(src_ix[k][:, :], core.other_idx[:, bass.ds(g * T, T)]).then_inc(ix_ok, 1)
                    nc.gpsimd.tensor_copy(dst_ix[k][:, :], core.node_idx[:, bass.ds(g * T, T)]).then_inc(ix_ok, 1)
                    pool.wait_ge(ix_ok, 2 * g + 2)
                    pool.nop(nofuse=True)
                    for t in range(T):
                        pool.indirect_dma_start(kv[k][:, t, :], None, core.kv_rows,
                                                bass.IndirectOffsetOnAxis(ap=src_ix[k][:, t:t + 1], axis=0)).then_inc(g_in[k], 16)
                        pool.indirect_dma_start(q[k][:, t, :], None, core.q_rows,
                                                bass.IndirectOffsetOnAxis(ap=dst_ix[k][:, t:t + 1], axis=0)).then_inc(g_in[k], 16)
            halves(pool, body)

        @block.tensor
        def _(pe):
            pe.wait_ge(wts, 16)

            def turn_logits(g, k):
                pe.wait_ge(log_ok, g + 1)
                reached(pe, logc_ok, g - 1)
                for t in range(T):
                    last = nc.tensor.transpose(bank[4 + k][0:H, t * P:(t + 1) * P], logits[k][:, t, :], ident[:, :])
                last.then_inc(log_t, 1)

            def body(i):
                for k in range(2):
                    g = 2 * i + k
                    pe.wait_ge(a_in[k], 16 * (i + 1))
                    reached(pe, a_ok, g - 1)
                    pe.nop(nofuse=True)
                    for t in range(T):
                        last = nc.tensor.transpose(bank[k][0:ED, t * P:(t + 1) * P], attr[k][:, t, :], ident[:, :])
                    last.then_inc(a_t, 1)
                    pe.wait_ge(a_ok, g + 1)
                    reached(pe, sum_ok, g - 1)
                    for t in range(T):
                        last = nc.tensor.matmul(bank[2 + k][:, t * P:(t + 1) * P], attr_cols[k][:, t * P:(t + 1) * P], w_e[:, :],
                                                start=True, stop=True)
                    last.then_inc(e_mm, 1)
                    if not (isinstance(i, int) and i == 0 and k == 0):
                        turn_logits(2 * i + k - 1, 1 - k)
            halves(pe, body)
            turn_logits(NG - 1, 1)

        @block.scalar
        def _(act):
            def logit_copy(g, k, i):
                act.wait_ge(log_t, g + 1)
                reached(act, st_l[k], 32 * i)
                nc.scalar.activation(logit_c[k][:, :], bank[4 + k][0:H, :], ACT.Copy, scale=float(C) ** -0.5).then_inc(logc_ok, 1)
                nc.scalar.activation(brk[k][:, :], core.same[0:H, bass.ds(g * GR, GR)], ACT.Copy, scale=BIG, bias=-BIG).then_inc(brk_ok, 1)

            def body(i):
                for k in range(2):
                    g = 2 * i + k
                    act.wait_ge(a_t, g + 1)
                    reached(act, e_mm, g - 1)
                    nc.scalar.activation(attr_cols[k][:, :], bank[k][0:ED, :], ACT.Copy).then_inc(a_ok, 1)
                    if k == 1:
                        logit_copy(2 * i, 0, i)
                    elif not (isinstance(i, int) and i == 0):
                        logit_copy(2 * i - 1, 1, i - 1)
            halves(act, body)
            logit_copy(NG - 1, 1, HALF - 1)

        @block.vector
        def _(dve):
            for k in range(2):
                nc.vector.memset(attr[k][:, :, :], 0.0).then_inc(zeroed, 1)

            def scan(g, k, i):
                start = -BIG if isinstance(g, int) and g == 0 else runmax[1 - k][:, GR - 1:GR]
                dve.wait_ge(logc_ok, g + 1)
                dve.wait_ge(brk_ok, g + 1)
                reached(dve, st_l[k], 32 * i)
                reached(dve, max_ok, g)
                nc.vector.tensor_tensor_scan(runmax[k][:, :], brk[k][:, :], logit_c[k][:, :], start, ALU.add, ALU.max).then_inc(max_ok, 1)

            def body(i):
                for k in range(2):
                    g = 2 * i + k
                    dve.wait_ge(g_in[k], 128 * (i + 1))
                    dve.wait_ge(e_mm, g + 1)
                    reached(dve, st_v[k], 16 * i)
                    reached(dve, prod_ok, g - 1)
                    e_rows = bank[2 + k][:, :].rearrange("p (t f) -> p t f", t=T).unsqueeze(2).broadcast_to([P, T, 2, D])
                    nc.vector.tensor_tensor(kv_e[k][:, :, :, :], kv[k][:, :, :].rearrange("p t (a f) -> p t a f", a=2), e_rows, ALU.add).then_inc(sum_ok, 1)
                    dve.wait_ge(sum_ok, g + 1)
                    reached(dve, log_ok, g - 1)
                    nc.vector.tensor_tensor(prod[k][:, :, :], q[k][:, :, :], kv_e[k][:, :, 0, :], ALU.mult).then_inc(prod_ok, 1)
                    dve.wait_ge(prod_ok, g + 1)
                    reached(dve, log_t, g - 1)
                    nc.vector.tensor_reduce(logits[k][:, :, :].rearrange("p t h -> p (t h)"),
                                            prod[k][:, :, :].rearrange("p t (h c) -> p (t h) c", h=H), AXX, ALU.add).then_inc(log_ok, 1)
                    if k == 1:
                        scan(2 * i, 0, i)
                    elif not (isinstance(i, int) and i == 0):
                        scan(2 * i - 1, 1, i - 1)
            halves(dve, body)
            scan(NG - 1, 1, HALF - 1)


def softmax_weights(core):
    nc = core.nc
    W = 7 * GR
    STEPS = NP // W
    assert STEPS % 2 == 0 and STEPS * W == NP
    with ExitStack() as s:
        def two(name, dt=F32):
            return [s.enter_context(nc.sbuf_tensor(f"{name}{k}", [H, W], dt)) for k in range(2)]
        logit, runmax, top = (two("sw_" + n) for n in ("logit", "runmax", "top"))
        brk = s.enter_context(nc.sbuf_tensor("sw_break", [H, W], F32))
        ld, st = ([core.sem(f"sw_{n}{k}") for k in range(2)] for n in ("in", "stored"))
        brk_ok, top_ok, diff_ok, ex_ok = (core.sem("sw_" + n) for n in ("break_ready", "top_ready", "diff_ready", "exp_ready"))
        block = s.enter_context(nc.Block())
        low = lambda n: NP - (n + 1) * W

        @block.sync
        def _(sp):
            for n in range(STEPS + 1):
                if n < STEPS:
                    reached(sp, st[n % 2], 16 * (n // 2))
                    sp.dma_start(logit[n % 2][:, :], core.logit_cols[:, low(n):low(n) + W]).then_inc(ld[n % 2], 16)
                    sp.dma_start(runmax[n % 2][:, :], core.runmax_cols[:, low(n):low(n) + W]).then_inc(ld[n % 2], 16)
                if n:
                    sp.wait_ge(ex_ok, n)
                    sp.dma_start(core.exp_cols[:, low(n - 1):low(n - 1) + W], logit[(n - 1) % 2][:, :]).then_inc(st[(n - 1) % 2], 16)
            for k in range(2):
                sp.wait_ge(st[k], 16 * (STEPS // 2))

        @block.scalar
        def _(act):
            def breaks(n):
                reached(act, top_ok, n)
                nc.scalar.activation(brk[:, :], core.same[0:H, low(n) + 1:low(n) + 1 + W], ACT.Copy, scale=BIG, bias=-BIG).then_inc(brk_ok, 1)
            breaks(0)
            for n in range(STEPS):
                if n + 1 < STEPS:
                    breaks(n + 1)
                act.wait_ge(diff_ok, n + 1)
                nc.scalar.activation(logit[n % 2][:, :], logit[n % 2][:, :], ACT.Exp).then_inc(ex_ok, 1)

        @block.vector
        def _(dve):
            for n in range(STEPS):
                k = n % 2
                dve.wait_ge(ld[k], 32 * (n // 2 + 1))
                dve.wait_ge(brk_ok, n + 1)
                reached(dve, top_ok, n)
                nc.vector.tensor_tensor_scan(top[k][:, ::-1], brk[:, ::-1], runmax[k][:, ::-1],
                                             top[1 - k][:, 0:1] if n else -BIG, ALU.add, ALU.max).then_inc(top_ok, 1)
                dve.wait_ge(top_ok, n + 1)
                nc.vector.tensor_tensor(logit[k][:, :], logit[k][:, :], top[k][:, :], ALU.subtract).then_inc(diff_ok, 1)


def weighted_sums(core):
    nc, bank, ident = core.nc, core.bank, core.ident
    with ExitStack() as s:
        def sb(name, shape, dt=F32):
            return s.enter_context(nc.sbuf_tensor(name, shape, dt))

        def two(name, shape, dt=F32):
            return [sb(f"{name}{k}", shape, dt) for k in range(2)]
        end_ix, vj, ex = two("ws_end_ix", [P, T], I32), two("ws_vj", [P, T, D]), two("ws_exp", [H, GR])
        wv, num, den = two("ws_weighted", [P, T, D]), two("ws_num", [D, GR]), two("ws_den", [H, GR])
        inv, rows = two("ws_inv", [P, T * H]), two("ws_rows", [P, T, D])
        ix_ok = core.sem("ws_index_ready")
        ld, sc_out = ([core.sem(f"ws_{n}{k}") for k in range(2)] for n in ("in", "scattered"))
        ex_t, wv_ok, wv_t, num_ok, den_ok, num_t, cap_ok, inv_ok, rows_ok = (core.sem("ws_" + n) for n in (
            "exp_transposed", "weighted_ready", "weighted_transposed", "num_ready", "den_ready", "sums_transposed",
            "den_guarded", "inverse_ready", "rows_ready"))
        block = s.enter_context(nc.Block())

        @block.sync
        def _(sp):
            def body(i):
                for k in range(2):
                    g = 2 * i + k
                    reached(sp, den_ok, g - 1)
                    sp.dma_start(vj[k][:, :, :], core.vj_rows[bass.ds(g * GR, GR), :].rearrange("(t p) f -> p t f", p=P)).then_inc(ld[k], 16)
                    sp.dma_start(ex[k][:, :], core.exp_cols[:, bass.ds(g * GR, GR)]).then_inc(ld[k], 16)
            halves(sp, body)
            for k in range(2):
                sp.wait_ge(sc_out[k], 64 * HALF)

        @block.gpsimd
        def _(pool):
            def body(i):
                for k in range(2):
                    reached(pool, sc_out[k], 64 * i)
                    pool.nop(nofuse=True)
                    nc.gpsimd.tensor_copy(end_ix[k][:, :], core.end_idx[:, bass.ds((2 * i + k) * T, T)]).then_inc(ix_ok, 1)
                    pool.wait_ge(ix_ok, 2 * i + k + 1)
                    pool.wait_ge(rows_ok, 2 * i + k + 1)
                    pool.nop(nofuse=True)
                    for t in range(T):
                        pool.indirect_dma_start(core.conv_rows, bass.IndirectOffsetOnAxis(ap=end_ix[k][:, t:t + 1], axis=0),
                                                rows[k][:, t, :], None, bounds_check=NP - 1, oob_is_err=False).then_inc(sc_out[k], 16)
            halves(pool, body)

        @block.tensor
        def _(pe):
            def back(g, k):
                pe.wait_ge(num_ok, g + 1)
                pe.wait_ge(den_ok, g + 1)
                reached(pe, rows_ok, g - 1)
                for t in range(T):
                    nc.tensor.transpose(bank[4 + k][:, t * P:(t + 1) * P], num[k][:, t * P:(t + 1) * P], ident[:, :])
                for t in range(T):
                    last = nc.tensor.transpose(bank[6 + k][:, t * H:(t + 1) * H], den[k][:, t * P:(t + 1) * P], ident[0:H, 0:H])
                last.then_inc(num_t, 1)

            def body(i):
                for k in range(2):
                    g = 2 * i + k
                    pe.wait_ge(ld[k], 32 * (i + 1))
                    reached(pe, wv_ok, g - 1)
                    pe.nop(nofuse=True)
                    for t in range(T):
                        last = nc.tensor.transpose(bank[k][:, t * H:(t + 1) * H], ex[k][:, t * P:(t + 1) * P], ident[0:H, 0:H])
                    last.then_inc(ex_t, 1)
                    if not (isinstance(i, int) and i == 0 and k == 0):
                        back(2 * i + k - 1, 1 - k)
                    pe.wait_ge(wv_ok, g + 1)
                    reached(pe, num_ok, g - 1)
                    for t in range(T):
                        last = nc.tensor.transpose(bank[2 + k][:, t * P:(t + 1) * P], wv[k][:, t, :], ident[:, :])
                    last.then_inc(wv_t, 1)
            halves(pe, body)
            back(NG - 1, 1)

        @block.vector
        def _(dve):
            def divide(g, k, i):
                dve.wait_ge(num_t, g + 1)
                reached(dve, rows_ok, g - 1)
                nc.vector.tensor_scalar(inv[k][:, :], bank[6 + k][:, 0:T * H], 1e-30, None, ALU.max).then_inc(cap_ok, 1)
                dve.wait_ge(cap_ok, g + 1)
                nc.vector.reciprocal(inv[k][:, :], inv[k][:, :]).then_inc(inv_ok, 1)
                dve.wait_ge(inv_ok, g + 1)
                reached(dve, sc_out[k], 64 * i)
                nc.vector.tensor_tensor(rows[k][:, :, :].rearrange("p t (h c) -> p (t h) c", h=H),
                                        bank[4 + k][:, :].rearrange("p (n c) -> p n c", c=C),
                                        inv[k][:, :].unsqueeze(2).broadcast_to([P, T * H, C]), ALU.mult).then_inc(rows_ok, 1)

            def body(i):
                for k in range(2):
                    g = 2 * i + k
                    first = isinstance(g, int) and g == 0
                    dve.wait_ge(ex_t, g + 1)
                    dve.wait_ge(ld[k], 32 * (i + 1))
                    reached(dve, wv_t, g - 1)
                    nc.vector.tensor_tensor(wv[k][:, :, :].rearrange("p t (h c) -> p (t h) c", h=H),
                                            vj[k][:, :, :].rearrange("p t (h c) -> p (t h) c", h=H),
                                            bank[k][:, 0:T * H].unsqueeze(2).broadcast_to([P, T * H, C]), ALU.mult).then_inc(wv_ok, 1)
                    reached(dve, num_t, g - 1)
                    reached(dve, den_ok, g)
                    nc.vector.tensor_tensor_scan(den[k][:, :], core.same[0:H, bass.ds(g * GR, GR)], ex[k][:, :],
                                                 0.0 if first else den[1 - k][:, GR - 1:GR], ALU.mult, ALU.add).then_inc(den_ok, 1)
                    dve.wait_ge(wv_t, g + 1)
                    reached(dve, num_ok, g)
                    nc.vector.tensor_tensor_scan(num[k][:, :], core.same[:, bass.ds(g * GR, GR)], bank[2 + k][:, :],
                                                 0.0 if first else num[1 - k][:, GR - 1:GR], ALU.mult, ALU.add).then_inc(num_ok, 1)
                    if k == 1:
                        divide(2 * i, 0, i)
                    elif not (isinstance(i, int) and i == 0):
                        divide(2 * i - 1, 1, i - 1)
            halves(dve, body)
            divide(NG - 1, 1, HALF - 1)


def feed_forward(core, w, out):
    nc, bank, ident = core.nc, core.bank, core.ident
    FC = F // P
    with ExitStack() as s:
        def sb(name, shape, dt=F32):
            return s.enter_context(nc.sbuf_tensor(name, shape, dt))

        def two(name, shape, dt=F32):
            return [sb(f"{name}{k}", shape, dt) for k in range(2)]
        w1, w2 = sb("ff_w1", [D, F]), sb("ff_w2", [P, FC, D])
        g1, b1, bf1, bf2 = sb("ff_g1", [D, 1]), sb("ff_b1", [D, 1]), sb("ff_bf1", [P, FC]), sb("ff_bf2", [D, 1])
        g2, b2 = sb("ff_g2", [P, D]), sb("ff_b2", [P, D])
        agg, skip, x1 = two("ff_agg", [P, T, D]), two("ff_skip", [P, T, D]), two("ff_x1", [P, T, D])
        y, xh, h_c = two("ff_y", [P, T, D]), two("ff_xhat", [P, T, D]), two("ff_h_cols", [D, GR])
        act_c = [sb(f"ff_gelu{c}", [P, GR]) for c in range(FC)]
        z_c, zn, u, v, fin = two("ff_z_cols", [D, GR]), two("ff_zn", [P, T, D]), two("ff_u", [P, T, D]), two("ff_v", [P, T, D]), two("ff_out", [P, T, D])
        stats = [two(f"ff_stats{n}_", [P, T, 6]) for n in range(3)]
        mom = [two(f"ff_moments{n}_", [P, T, 2]) for n in range(3)]
        epv = [two(f"ff_eps_var{n}_", [P, T]) for n in range(3)]
        rstd = [two(f"ff_rstd{n}_", [P, T]) for n in range(3)]
        half = sb("ff_half", [P, T])
        wts, half_ok = core.sem("ff_weights_in"), core.sem("ff_half_ready")
        ld, st = ([core.sem(f"ff_{n}{k}") for k in range(2)] for n in ("in", "stored"))
        names = ("y_chain", "xhat_ready", "xhat_transposed", "h_cols_ready", "hidden_product", "gelu_ready", "out_product",
                 "z_cols_ready", "z_transposed", "z_chain", "zn_ready", "u_ready", "v_ready", "out_ready", "v_chain")
        y_c, xh_ok, xh_t, h_ok, f1, ge, f2, z_ok, z_t, z_c_s, zn_ok, u_ok, v_ok, fin_ok, v_c = (core.sem("ff_" + n) for n in names)
        mom_ok, pow_c, rstd_ok = ([core.sem(f"ff_{n}{m}") for m in range(3)] for n in ("moments_ready", "pow_chain", "rstd_ready"))
        block = s.enter_context(nc.Block())

        @block.sync
        def _(sp):
            with nc.allow_non_contiguous_dma(reason="bias values, one per partition"):
                sp.dma_start(w1[:, :], w["Wf1"]).then_inc(wts, 16)
                sp.dma_start(w2[:, :, :], w["Wf2"].rearrange("(c p) f -> p c f", p=P)).then_inc(wts, 16)
                for tile, name in ((g1, "g1"), (b1, "b1"), (bf2, "bf2")):
                    sp.dma_start(tile[:, :], w[name].rearrange("(p a) -> p a", a=1)).then_inc(wts, 16)
                sp.dma_start(bf1[:, :], w["bf1"].rearrange("(c p) -> p c", p=P)).then_inc(wts, 16)
                sp.dma_start(g2[:, :], w["g2"].partition_broadcast(P)).then_inc(wts, 16)
                sp.dma_start(b2[:, :], w["b2"].partition_broadcast(P)).then_inc(wts, 16)

            def rows(t, g):
                return t[bass.ds(g * GR, GR), :].rearrange("(p k) f -> p k f", k=T)

            def load(g, k):
                reached(sp, v_ok, g - 1)
                sp.dma_start(agg[k][:, :, :], rows(core.conv_rows, g)).then_inc(ld[k], 16)
                sp.dma_start(skip[k][:, :, :], rows(core.skip_rows, g)).then_inc(ld[k], 16)
                sp.dma_start(x1[k][:, :, :], rows(core.x1_rows, g)).then_inc(ld[k], 16)

            def store(g, k):
                reached(sp, fin_ok, g + 1)
                if isinstance(g, int) and g == NG - 1:
                    sp.dma_start(out[g * GR:N, :].rearrange("(p k) f -> p k f", k=T), fin[k][0:LAST, :, :]).then_inc(st[k], 16)
                else:
                    sp.dma_start(rows(out, g), fin[k][:, :, :]).then_inc(st[k], 16)

            def body(i):
                for k in range(2):
                    load(2 * i + k, k)
                for k in range(2):
                    if not (isinstance(i, int) and i == 0):
                        store(2 * i - 2 + k, k)
            halves(sp, body)
            for k in range(2):
                store(NG - 2 + k, k)
            for k in range(2):
                sp.wait_ge(st[k], 16 * HALF)

        @block.tensor
        def _(pe):
            pe.wait_ge(wts, 8 * 16)

            def turn_z(g, k):
                pe.wait_ge(z_ok, g + 1)
                reached(pe, zn_ok, g)
                for t in range(T):
                    last = nc.tensor.transpose(bank[7][:, t * P:(t + 1) * P], z_c[k][:, t * P:(t + 1) * P], ident[:, :])
                last.then_inc(z_t, 1)

            def body(i):
                for k in range(2):
                    g = 2 * i + k
                    pe.wait_ge(xh_ok, g + 1)
                    reached(pe, h_ok, g)
                    for t in range(T):
                        last = nc.tensor.transpose(bank[0][:, t * P:(t + 1) * P], xh[k][:, t, :], ident[:, :])
                    last.then_inc(xh_t, 1)
                    if not (isinstance(i, int) and i == 0 and k == 0):
                        turn_z(2 * i + k - 1, 1 - k)
                    pe.wait_ge(h_ok, g + 1)

                    def hidden(c):
                        reached(pe, ge, FC * g + c - 2)
                        nc.tensor.matmul(bank[1 + c % 2][:, :], w1[:, c * P:(c + 1) * P], h_c[k][:, :], start=True, stop=True).then_inc(f1, 1)

                    def output(c):
                        pe.wait_ge(ge, FC * g + c + 1)
                        if c == 0:
                            reached(pe, z_ok, g - 1)
                        m = nc.tensor.matmul(bank[3 + k][:, :], w2[:, c, :], act_c[c][:, :], start=(c == 0), stop=(c == FC - 1))
                        return m
                    hidden(0)
                    hidden(1)
                    output(0)
                    hidden(2)
                    output(1)
                    hidden(3)
                    output(2)
                    output(3).then_inc(f2, 1)
            halves(pe, body)
            turn_z(NG - 1, 1)

        @block.scalar
        def _(act):
            act.wait_ge(wts, 8 * 16)

            def body(i):
                for k in range(2):
                    g = 2 * i + k
                    act.wait_ge(xh_t, g + 1)
                    reached(act, z_ok, g - 1)
                    nc.scalar.activation(h_c[k][:, :], bank[0][:, :], ACT.Identity, bias=b1[:, 0:1], scale=g1[:, 0:1]).then_inc(h_ok, 1)
                    for c in range(FC):
                        act.wait_ge(f1, FC * g + c + 1)
                        if c == 0:
                            reached(act, f2, g)
                        nc.scalar.activation(act_c[c][:, :], bank[1 + c % 2][:, :], ACT.Gelu, bias=bf1[:, c:c + 1]).then_inc(ge, 1)
            halves(act, body)

        @block.gpsimd
        def _(pool):
            nc.gpsimd.memset(half[:, :], -0.5).then_inc(half_ok, 1)
            pool.wait_ge(half_ok, 1)
            used = (xh_ok, zn_ok, fin_ok)

            def power(m, g, k):
                pool.wait_ge(mom_ok[m], g + 1)
                reached(pool, used[m], g - 1)
                inverse_deviation(nc, pool, pow_c[m], g, mom[m][k], epv[m][k], half, rstd[m][k]).then_inc(rstd_ok[m], 1)

            def body(i):
                for k in range(2):
                    power(0, 2 * i + k, k)
                    if not (isinstance(i, int) and i == 0 and k == 0):
                        power(1, 2 * i + k - 1, 1 - k)
                        power(2, 2 * i + k - 1, 1 - k)
            halves(pool, body)
            power(1, NG - 1, 1)
            power(2, NG - 1, 1)

        @block.vector
        def _(dve):
            dve.wait_ge(wts, 8 * 16)

            def normalize(m, src, dst, k, ready, g):
                dve.wait_ge(mom_ok[m], g + 1)
                dve.wait_ge(rstd_ok[m], g + 1)
                for t in range(T):
                    last = nc.vector.tensor_scalar(dst[:, t, :], src[:, t, :], mom[m][k][:, t, 0:1], rstd[m][k][:, t:t + 1],
                                                   ALU.subtract, ALU.mult)
                last.then_inc(ready, 1)

            def tail(g, k, i):
                dve.wait_ge(f2, g + 1)
                dve.wait_ge(h_ok, g + 1)
                reached(dve, z_t, g - 1)
                nc.vector.scalar_tensor_tensor(out=z_c[k][:, :], in0=bank[3 + k][:, :], scalar=bf2[:, 0:1], in1=h_c[k][:, :],
                                               op0=ALU.add, op1=ALU.add).then_inc(z_ok, 1)
                z_rows = bank[7][:, :].rearrange("p (t f) -> p t f", t=T)
                dve.wait_ge(z_t, g + 1)
                reached(dve, rstd_ok[1], g - 1)
                norm_stats(nc, dve, z_c_s, g, z_rows, stats[1][k], mom[1][k]).then_inc(mom_ok[1], 1)
                reached(dve, u_ok, g - 1)
                normalize(1, z_rows, zn[k], k, zn_ok, g)
                dve.wait_ge(zn_ok, g + 1)
                reached(dve, v_ok, g - 1)
                nc.vector.tensor_tensor(u[k][:, :, :], zn[k][:, :, :], g2[:, :].unsqueeze(1).broadcast_to([P, T, D]), ALU.mult).then_inc(u_ok, 1)
                dve.wait_ge(u_ok, g + 1)
                nc.vector.tensor_tensor(u[k][:, :, :], u[k][:, :, :], b2[:, :].unsqueeze(1).broadcast_to([P, T, D]), ALU.add).then_inc(v_c, 1)
                dve.wait_ge(v_c, 2 * g + 1)
                reached(dve, fin_ok, g - 1)
                nc.vector.tensor_tensor(v[k][:, :, :], u[k][:, :, :], x1[k][:, :, :], ALU.add).then_inc(v_ok, 1)
                dve.wait_ge(v_ok, g + 1)
                reached(dve, rstd_ok[2], g - 1)
                norm_stats(nc, dve, v_c, 2 * g + 1, v[k], stats[2][k], mom[2][k]).then_inc(mom_ok[2], 1)
                reached(dve, st[k], 16 * i)
                normalize(2, v[k], fin[k], k, fin_ok, g)

            def body(i):
                for k in range(2):
                    g = 2 * i + k
                    dve.wait_ge(ld[k], 48 * (i + 1))
                    reached(dve, xh_ok, g - 1)
                    nc.vector.tensor_tensor(y[k][:, :, :], agg[k][:, :, :], skip[k][:, :, :], ALU.add).then_inc(y_c, 1)
                    dve.wait_ge(y_c, 2 * g + 1)
                    reached(dve, rstd_ok[0], g - 1)
                    norm_stats(nc, dve, y_c, 2 * g + 1, y[k], stats[0][k], mom[0][k]).then_inc(mom_ok[0], 1)
                    reached(dve, xh_t, g - 1)
                    normalize(0, y[k], xh[k], k, xh_ok, g)
                    if k == 1:
                        tail(2 * i, 0, i)
                    elif not (isinstance(i, int) and i == 0):
                        tail(2 * i - 1, 1, i - 1)
            halves(dve, body)
            tail(NG - 1, 1, HALF - 1)


def build(nc, a, out):
    with ExitStack() as ctx:
        core = Core(nc, ctx)
        l1 = {name[7:]: ap for name, ap in a.items() if name.startswith("L1_gnn_")}
        make_identity(core)
        core.end_stage()
        sort_by_src(core, a["dst"], a["src"])
        core.end_stage()

        def by_src(sp, here, after, other, sem):
            return load_blocks(sp, here, core.by_src, NP, 0, sem) + load_blocks(sp, after, core.by_src, NP, 1, sem)

        def by_dst(sp, here, after, other, sem):
            return (load_blocks(sp, here, a["dst"], E, 0, sem) + load_blocks(sp, after, a["dst"], E, 1, sem)
                    + load_blocks(sp, other, a["src"], E, 0, sem))
        index_tables(core, "mpx_", by_src, True, (core.agg_rows, core.msg_rows[NP:2 * NP, :]),
                     core.by_src.rearrange("(u e) w -> u e w", u=HALF)[:, 0, 0].rearrange("(a u) -> a u", a=1))
        core.end_stage()
        message_passing(core, a["x"], a["L0_gnn_W_edge"], a["L0_gnn_b_edge"], a["L0_gnn_W_agg"], a["L0_gnn_b_agg"])
        core.end_stage()
        index_tables(core, "atx_", by_dst, False, (core.conv_rows,))
        core.end_stage()
        project_nodes(core, a["x"], l1, l1)
        core.end_stage()
        edge_logits(core, a["edge_attr_64"], l1["We"])
        core.end_stage()
        softmax_weights(core)
        core.end_stage()
        weighted_sums(core)
        core.end_stage()
        feed_forward(core, l1, out)


def kernel(**inputs):
    import numpy as np
    import concourse.bacc as bacc
    from concourse.bass_utils import run_bass_kernel_spmd as run

    nc = bacc.Bacc("TRN2", target_bir_lowering=False, num_devices=1)
    arrays, aps = {}, {}
    for name, value in inputs.items():
        value = np.ascontiguousarray(value)
        arrays["in_" + name] = value
        aps[name] = nc.dram_tensor("in_" + name, value.shape, mybir.dt.from_np(value.dtype), kind="ExternalInput").ap()
    out = nc.dram_tensor("out_rows", (N, D), F32, kind="ExternalOutput").ap()
    build(nc, aps, out)
    return run(nc, [arrays], core_ids=[0]).results[0]["out_rows"]
```

```python
import concourse.bass as bass
from concourse import mybir
from contextlib import ExitStack

F32 = mybir.dt.float32
BF16 = mybir.dt.bfloat16
I32 = mybir.dt.int32
ALU = mybir.AluOpType
ACT = mybir.ActivationFunctionType
AXX = mybir.AxisListType.X

P = 128
N = 50000
E = 50000
D = 128
ED = 64
H = 8
C = D // H
F = 4 * D
LAYERS = 3
T = 4
GR = T * P
NG = -(-N // GR)
NP = NG * GR
NT = NG * T
HALF = NG // 2
LAG = 4
BEHIND = 2
LAST = (N - (NG - 1) * GR) // T
PAD_DST = 60000
FAR = 65536
BIG = 3.0e38
EPS = 1e-5
HEAD_SHIFT = (2 * GR).bit_length() - 1
assert NG % 2 == 0 and (N - (NG - 1) * GR) % T == 0 and N == E


def reached(eng, sem, count, base=0):
    if isinstance(count, int) and count <= 0:
        return
    eng.wait_ge(sem, base + count)
    if eng.engine == mybir.EngineType.SP:
        eng.nop(nofuse=True)


def halves(eng, body):
    body(0)
    body(1)
    with eng.Fori(2, HALF) as i:
        body(i)


def turns(eng, turn):
    def straight(n):
        def do(lag, step):
            if 0 <= n + lag < NG:
                step(n + lag, (n + lag) % 2, (n + lag) // 2)
        turn(do)

    def looped(j, parity):
        turn(lambda lag, step: step(2 * j + parity + lag, (parity + lag) % 2, j + (parity + lag) // 2))
    for n in range(-LAG, LAG):
        straight(n)
    with eng.Fori(LAG // 2, (NG - LAG) // 2) as j:
        looped(j, 0)
        looped(j, 1)
    for n in range((NG - LAG) // 2 * 2, NG + LAG):
        straight(n)


def rows_of_group(t, g, width):
    return t[bass.ds(g * GR, GR), :].rearrange("(p k) f -> p (k f)", k=T)


class Core:

    def __init__(self, nc, ctx):
        self.nc, self.ctx = nc, ctx

        def dram(name, shape, dt):
            return nc.dram_tensor(name, shape, dt, kind="Internal").ap()

        self.h_cols = dram("h_cols", [D, NP], F32)
        self.msg_rows = dram("msg_rows", [2 * NP, D], F32)
        self.agg_rows = dram("agg_rows", [NP, D], F32)
        self.conv_rows = dram("conv_rows", [NP, D], F32)
        self.same_row = dram("same_row", [1, NP + 1], BF16)
        self.by_low = dram("by_low", [NP, 2], I32)
        self.by_src = dram("by_src", [NP, 2], I32)
        self.kv_rows = dram("kv_rows", [NP, 2 * D], F32)
        self.q_rows = dram("q_rows", [NP, D], F32)
        self.skip_rows = dram("skip_rows", [NP, D], F32)
        self.x1_rows = dram("x1_rows", [NP, D], F32)
        self.same = ctx.enter_context(nc.sbuf_tensor("same", [P, NP], BF16))
        self.other_idx = ctx.enter_context(nc.sbuf_tensor("other_idx", [P, 2 * NT], I32))
        self.node_idx = ctx.enter_context(nc.sbuf_tensor("node_idx", [P, NT], I32))
        self.end_idx = ctx.enter_context(nc.sbuf_tensor("end_idx", [P, NT], I32))
        self.nodes_done = ctx.enter_context(nc.sbuf_tensor("nodes_done", [1, HALF + 8], I32))
        self.ident = ctx.enter_context(nc.sbuf_tensor("ident", [P, P], F32))
        self.earlier = ctx.enter_context(nc.sbuf_tensor("earlier", [P, P], BF16))
        self.not_earlier = ctx.enter_context(nc.sbuf_tensor("not_earlier", [P, P], BF16))
        self.ones = ctx.enter_context(nc.sbuf_tensor("ones", [P, P], BF16))
        self.digits = ctx.enter_context(nc.sbuf_tensor("digits", [P, LOW], BF16))
        self.bank = [ctx.enter_context(nc.psum_tensor(f"bank{b}", [P, 512], F32)) for b in range(8)]

        self.sems = []

    def flags(self, g, groups):
        part = bass.ds(g * GR, groups * GR)
        return self.same[:, part], self.same_row[0, part].partition_broadcast(P)

    def sem(self, name):
        self.sems.append(self.nc.alloc_semaphore(name=name))
        return self.sems[-1]

    def end_stage(self):
        self.nc.clear_and_free_semaphores(self.sems)
        self.nc.all_engine_barrier()
        self.sems = []


FULL = E // (P * P) * P * P
NB = FULL // (P * P)
LOW, HIGH = 256, 256
assert NP <= LOW * HIGH and NB + 1 == T


def load_blocks(sp, tile, vec, count, shift, sem):
    mid = (count - FULL - shift) // P
    rest = count - FULL - shift - mid * P
    tail = "" if len(vec.shape) == 1 else " w"
    sp.dma_start(tile[:, 0:NB], vec[shift:shift + FULL].rearrange(f"(b j p){tail} -> j b p{tail}", b=NB, p=P)).then_inc(sem, 16)
    at = FULL + shift
    sp.dma_start(tile[0:mid, NB], vec[at:at + mid * P].rearrange(f"(j p){tail} -> j p{tail}", p=P)).then_inc(sem, 16)
    if rest:
        sp.dma_start(tile[mid:mid + 1, NB, 0:rest], vec[at + mid * P:count].rearrange(f"(a p){tail} -> a p{tail}", a=1)).then_inc(sem, 16)
    return 2 + bool(rest)


def make_identity(core):
    nc = core.nc
    done = core.sem("mask_step")
    with nc.Block() as block:
        @block.gpsimd
        def _(pool):
            pool.memset(core.ident[:, :], 0.0).then_inc(done, 1)
            pool.memset(core.earlier[:, :], 1.0).then_inc(done, 1)
            pool.memset(core.not_earlier[:, :], 1.0).then_inc(done, 1)
            pool.memset(core.ones[:, :], 1.0).then_inc(done, 1)
            pool.iota(core.digits[:, :], pattern=[[1, LOW]], base=0, channel_multiplier=0,
                      allow_small_or_imprecise_dtypes=True).then_inc(done, 1)
            pool.wait_ge(done, 5)
            pool.affine_select(out=core.ident[:, :], in_=core.ident[:, :], compare_op=ALU.not_equal, fill=1.0,
                               base=0, pattern=[[-1, P]], channel_multiplier=1).then_inc(done, 1)
            pool.affine_select(out=core.earlier[:, :], in_=core.earlier[:, :], compare_op=ALU.is_gt, fill=0.0,
                               base=0, pattern=[[1, P]], channel_multiplier=-1).then_inc(done, 1)
            pool.affine_select(out=core.not_earlier[:, :], in_=core.not_earlier[:, :], compare_op=ALU.is_ge, fill=0.0,
                               base=0, pattern=[[-1, P]], channel_multiplier=1).then_inc(done, 1)


def sort_by_src(core, dst, src, x, W_edge):
    nc, bank = core.nc, core.bank
    with ExitStack() as s:
        def sb(name, shape, dt=F32):
            return s.enter_context(nc.sbuf_tensor(name, shape, dt))

        def two(name, shape, dt=F32):
            return [sb(f"{name}{k}", shape, dt) for k in range(2)]
        pair_i, digit_i = sb("so_pair_i", [P, T, P, 2], I32), two("so_digit_i", [P, T, P], I32)
        pair_f, digit_f = sb("so_pair_f", [P, 2, T, P]), two("so_digit_f", [P, T, P])
        table = two("so_digit_table", [P, NT])
        payload = sb("so_payload", [P, NT, 2], I32)
        ones_col, ones_row = sb("so_ones_col", [P, 1], BF16), sb("so_ones_row", [1, P])
        zero_row = sb("so_zero_row", [P, LOW], BF16)
        count, incl, base_row = two("so_count", [1, LOW]), two("so_incl", [1, LOW]), two("so_base", [1, LOW])
        onehot = two("so_onehot", [P, T, LOW], BF16)
        onehot_hi = two("so_onehot_hi", [P, T, LOW], BF16)
        picked = sb("so_picked", [P, LOW])
        w_edge, x_rows = sb("so_w_edge", [D, D]), two("so_x_rows", [P, GR])
        h_out, msg_out = two("so_h_out", [D, GR]), two("so_msg_out", [P, GR])
        CLEARS = 14
        zeros = sb("so_zeros", [P, NP * D // (CLEARS * P)])
        w_in, zero_ok, cleared, x_t = (core.sem("so_" + n) for n in ("w_edge_in", "zeros_ready", "rows_cleared", "x_transposed"))
        h0_ok, m0_mm, m0_ok = core.sem("so_h0_ready"), core.sem("so_m0_product"), core.sem("so_m0_ready")
        x_in, h0_st, m0_st = ([core.sem(f"so_{n}{k}") for k in range(2)] for n in ("x_in", "h0_stored", "m0_stored"))
        pos_f, pos_i, pay = two("so_pos_f", [P, T]), two("so_pos_i", [P, T], I32), two("so_pay", [P, T, 2], I32)

        def clear_part(rows, c):
            return rows.rearrange("(c p r) f -> c p (r f)", c=CLEARS, p=P)[c]

        for turn, to in enumerate((core.by_low, core.by_src)):
            n = f"so{turn}_"
            filled, loaded, dig, flt, tr, tab = (core.sem(n + x) for x in ("filled", "loaded", "digits", "floats", "transposed", "tables"))
            with nc.Block() as block:
                @block.sync
                def _(sp):
                    if turn == 0:
                        sp.wait_ge(filled, 2)
                        load_blocks(sp, digit_i[0], src, E, 0, loaded)
                        load_blocks(sp, digit_i[1], dst, E, 0, loaded)
                    else:
                        load_blocks(sp, pair_i, core.by_low, NP, 0, loaded)

                @block.vector
                def _(dve):
                    if turn == 0:
                        nc.vector.memset(digit_i[0][:, :, :], NP - 1).then_inc(filled, 1)
                        nc.vector.memset(digit_i[1][:, :, :], 0).then_inc(filled, 1)
                        nc.vector.memset(ones_col[:, :], 1.0)
                        nc.vector.memset(ones_row[:, :], 1.0)
                        nc.vector.memset(zero_row[:, :], 0.0)
                        dve.wait_ge(loaded, 96)
                        for c in range(2):
                            nc.vector.tensor_copy(pair_i[:, :, :, c], digit_i[c][:, :, :]).then_inc(dig, 1)
                    else:
                        dve.wait_ge(loaded, 32)
                        dve.sem_inc(dig, 2)
                    dve.wait_ge(dig, 2)
                    nc.vector.tensor_scalar(digit_i[0][:, :, :], pair_i[:, :, :, 0], LOW - 1, None, ALU.bitwise_and).then_inc(dig, 1)
                    nc.vector.tensor_scalar(digit_i[1][:, :, :], pair_i[:, :, :, 0], 8, None, ALU.logical_shift_right).then_inc(dig, 1)
                    dve.wait_ge(dig, 4)
                    for c in range(2):
                        nc.vector.tensor_copy(digit_f[c][:, :, :], digit_i[c][:, :, :]).then_inc(flt, 1)
                        nc.vector.tensor_copy(pair_f[:, c, :, :], pair_i[:, :, :, c]).then_inc(flt, 1)
                    dve.wait_ge(tr, 4)
                    for c in range(2):
                        nc.vector.tensor_copy(table[c][:, :], bank[c][:, 0:NT]).then_inc(tab, 1)
                        nc.vector.tensor_copy(payload[:, :, c], bank[2 + c][:, 0:NT]).then_inc(tab, 1)

                @block.tensor
                def _(pe):
                    pe.wait_ge(flt, 4)
                    for c, tile in enumerate((digit_f[0], digit_f[1], pair_f[:, 0], pair_f[:, 1])):
                        for b in range(T):
                            last = nc.tensor.transpose(bank[c][:, b * P:(b + 1) * P], tile[:, b, :], core.ident[:, :])
                        last.then_inc(tr, 1)

            if turn == 0:
                hot, cnt, hist, scan_ok, base_ok = (core.sem(n + x) for x in ("onehots", "counted", "counts", "inclusive", "bases"))
                with nc.Block() as block:
                    @block.sync
                    def _(sp):
                        sp.wait_ge(zero_ok, 1)
                        for c in range(CLEARS):
                            sp.dma_start(clear_part(core.agg_rows, c), zeros[:, :]).then_inc(cleared, 16)

                    @block.vector
                    def _(dve):
                        nc.vector.memset(zeros[:, :], 0.0).then_inc(zero_ok, 1)

                        def body(i):
                            for k in range(2):
                                g = 2 * i + k
                                reached(dve, cnt, g - 1)
                                for c, hots in enumerate((onehot, onehot_hi)):
                                    for t in range(T):
                                        last = nc.vector.tensor_scalar(hots[k][:, t, :], core.digits[:, :],
                                                                       table[c][:, bass.ds(g * T + t, 1)], None, ALU.is_equal)
                                last.then_inc(hot, 1)
                        halves(dve, body)
                        dve.wait_ge(cnt, NG)
                        for c in range(2):
                            nc.vector.tensor_copy(count[c][:, :], bank[c][0:1, 0:LOW]).then_inc(hist, 1)
                        dve.wait_ge(hist, 2)
                        for c in range(2):
                            nc.vector.tensor_tensor_scan(incl[c][:, :], count[c][:, :], count[c][:, :], 0.0, ALU.add, ALU.bypass).then_inc(scan_ok, 1)
                        dve.wait_ge(scan_ok, 2)
                        for c in range(2):
                            nc.vector.tensor_tensor(base_row[c][:, :], incl[c][:, :], count[c][:, :], ALU.subtract).then_inc(base_ok, 1)

                    @block.tensor
                    def _(pe):
                        for c in range(2):
                            nc.tensor.matmul(bank[c][0:1, 0:LOW], ones_col[:, :], zero_row[:, :], start=True, stop=True)

                        def body(i):
                            for k in range(2):
                                pe.wait_ge(hot, 2 * i + k + 1)
                                pe.nop(nofuse=True)
                                for t in range(T):
                                    for c, hots in enumerate((onehot, onehot_hi)):
                                        last = nc.tensor.matmul(bank[c][0:1, 0:LOW], ones_col[:, :], hots[k][:, t, :],
                                                                start=False, stop=True, skip_group_check=True)
                                last.then_inc(cnt, 1)
                        halves(pe, body)

            hot, v_ok, v_read, pos_ok, int_ok, pay_ok = (core.sem(n + x) for x in (
                "rank_onehots", "ranks_ready", "ranks_read", "positions", "position_ints", "payload_ready"))
            moved = [core.sem(f"{n}moved{k}") for k in range(2)]
            V = (bank[4][:, 0:LOW], bank[5][:, 0:LOW])
            with nc.Block() as block:
                @block.sync
                def _(sp):
                    if turn == 1:
                        for n, rows in enumerate((core.msg_rows[NP:2 * NP, :], core.conv_rows)):
                            for c in range(CLEARS):
                                sp.wait_ge(pay_ok, 3 * (n * CLEARS + c) + 1)
                                sp.dma_start(clear_part(rows, c), zeros[:, :]).then_inc(cleared, 16)
                        sp.wait_ge(cleared, 3 * CLEARS * 16)
                        return
                    sp.dma_start(w_edge[:, :], W_edge).then_inc(w_in, 16)

                    def load_x(g, k, i):
                        reached(sp, x_t, g - 1)
                        if isinstance(g, int) and g == NG - 1:
                            sp.dma_start(x_rows[k][0:LAST, :], x[g * GR:N, :].rearrange("(p k) f -> p (k f)", k=T)).then_inc(x_in[k], 16)
                        else:
                            sp.dma_start(x_rows[k][:, :], rows_of_group(x, g, D)).then_inc(x_in[k], 16)

                    def store_h(g, k, i):
                        reached(sp, h0_ok, g + 1)
                        sp.dma_start(core.h_cols[:, bass.ds(g * GR, GR)], h_out[k][:, :]).then_inc(h0_st[k], 16)

                    def store_messages(g, k, i):
                        reached(sp, m0_ok, g + 1)
                        sp.dma_start(rows_of_group(core.msg_rows, g, D), msg_out[k][:, :]).then_inc(m0_st[k], 16)

                    def step(do):
                        do(1, load_x)
                        do(0, store_h)
                        do(-3, store_messages)
                    turns(sp, step)
                    for k in range(2):
                        sp.wait_ge(h0_st[k], 16 * HALF)
                        sp.wait_ge(m0_st[k], 16 * HALF)

                @block.vector
                def _(dve):
                    def onehots(g, k, i):
                        reached(dve, v_ok, T * (g - 1) + 2)
                        for t in range(T):
                            last = nc.vector.tensor_scalar(onehot[k][:, t, :], core.digits[:, :],
                                                           table[turn][:, bass.ds(g * T + t, 1)], None, ALU.is_equal)
                        last.then_inc(hot, 1)

                    def pick(tiles):
                        def step(g, k, i):
                            for t in tiles:
                                dve.wait_ge(v_ok, T * g + t + 1)
                                if t == 0:
                                    reached(dve, int_ok, g - 1)
                                reached(dve, v_read, T * g + t)
                                nc.vector.tensor_tensor_reduce(out=picked[:, :], in0=onehot[k][:, t, :], in1=V[t % 2], scale=1.0, scalar=0.0,
                                                               op0=ALU.mult, op1=ALU.add, accum_out=pos_f[k][:, t:t + 1]).then_inc(v_read, 1)
                        return step

                    def positions(g, k, i):
                        dve.wait_ge(v_read, T * g + T)
                        reached(dve, moved[k], 64 * i)
                        nc.vector.tensor_copy(pos_i[k][:, :], pos_f[k][:, :]).then_inc(int_ok, 1)

                    def message_copy(g, k, i):
                        dve.wait_ge(m0_mm, g + 1)
                        reached(dve, m0_st[k], 16 * i)
                        nc.vector.tensor_copy(msg_out[k][:, :], bank[2 + k][:, :]).then_inc(m0_ok, 1)

                    def step(do):
                        do(0, pick((0, 1)))
                        do(1, onehots)
                        do(0, pick((2, 3)))
                        do(0, positions)
                        if turn == 0:
                            do(-2, message_copy)
                    turns(dve, step)

                @block.tensor
                def _(pe):
                    for v in V:
                        nc.tensor.matmul(v, ones_row[:, :], base_row[turn][:, :], start=True, stop=True)
                    if turn == 0:
                        pe.wait_ge(w_in, 16)

                    def ranks(tiles):
                        def step(g, k, i):
                            if 0 in tiles:
                                pe.wait_ge(hot, g + 1)
                                pe.nop(nofuse=True)
                            for t in tiles:
                                first = isinstance(g, int) and g == 0
                                reached(pe, v_read, T * g + t - 1)
                                two_before = onehot[k][:, t - 2, :] if t >= 2 else onehot[1 - k][:, T + t - 2, :]
                                one_before = onehot[k][:, t - 1, :] if t else onehot[1 - k][:, T - 1, :]
                                if not (first and t < 2):
                                    nc.tensor.matmul(V[t % 2], core.not_earlier[:, :], two_before, start=False, stop=True, skip_group_check=True)
                                if not (first and t < 1):
                                    nc.tensor.matmul(V[t % 2], core.ones[:, :], one_before, start=False, stop=True, skip_group_check=True)
                                nc.tensor.matmul(V[t % 2], core.earlier[:, :], onehot[k][:, t, :], start=False, stop=True,
                                                 skip_group_check=True).then_inc(v_ok, 1)
                        return step

                    def turn_x(g, k, i):
                        pe.wait_ge(x_in[k], 16 * (i + 1))
                        reached(pe, h0_ok, g - 1)
                        for t in range(T):
                            last = nc.tensor.transpose(bank[k][:, t * P:(t + 1) * P], x_rows[k][:, t * D:(t + 1) * D], core.ident[:, :])
                        last.then_inc(x_t, 1)

                    def messages(g, k, i):
                        pe.wait_ge(h0_ok, g + 1)
                        reached(pe, m0_ok, g - 1)
                        for t in range(T):
                            last = nc.tensor.matmul(bank[2 + k][:, t * P:(t + 1) * P], h_out[k][:, t * P:(t + 1) * P], w_edge[:, :],
                                                    start=True, stop=True)
                        last.then_inc(m0_mm, 1)

                    def step(do):
                        do(0, ranks((0, 1)))
                        if turn == 0:
                            do(0, turn_x)
                        do(0, ranks((2, 3)))
                        if turn == 0:
                            do(-1, messages)
                    turns(pe, step)

                @block.scalar
                def _(act):
                    def payloads(g, k, i):
                        reached(act, moved[k], 64 * i)
                        nc.scalar.activation(pay[k][:, :, :], payload[:, bass.ds(g * T, T), :], ACT.Copy).then_inc(pay_ok, 1)

                    def h_copy(g, k, i):
                        act.wait_ge(x_t, g + 1)
                        reached(act, h0_st[k], 16 * i)
                        reached(act, m0_mm, g - 1)
                        nc.scalar.activation(h_out[k][:, :], bank[k][:, :], ACT.Copy).then_inc(h0_ok, 1)

                    def step(do):
                        do(0, payloads)
                        if turn == 0:
                            do(0, h_copy)
                    turns(act, step)

                @block.gpsimd
                def _(pool):
                    def move(g, k, i):
                        pool.wait_ge(pay_ok, g + 1)
                        pool.wait_ge(int_ok, g + 1)
                        pool.nop(nofuse=True)
                        for t in range(T):
                            pool.indirect_dma_start(to, bass.IndirectOffsetOnAxis(ap=pos_i[k][:, t:t + 1], axis=0),
                                                    pay[k][:, t, :], None, bounds_check=NP - 1, oob_is_err=False).then_inc(moved[k], 16)

                    def step(do):
                        do(0, move)
                    turns(pool, step)
                    for k in range(2):
                        pool.wait_ge(moved[k], 64 * HALF)


def index_tables(core, name, load, paired, first_nodes=None):
    nc = core.nc
    with ExitStack() as s:
        def sb(nm, shape, dt):
            return s.enter_context(nc.sbuf_tensor(name + nm, shape, dt))
        wide = [P, T, P, 2] if paired else [P, T, P]
        here_t, after_t = sb("here_i", wide, I32), sb("after_i", wide, I32)
        other_t = None if paired else sb("other_i", wide, I32)
        here_i, after_i = ((t[:, :, :, 0] if paired else t[:, :, :]) for t in (here_t, after_t))
        other_i = here_t[:, :, :, 1] if paired else other_t[:, :, :]
        here_f, after_f, other_f = (sb(x, [P, T, P], F32) for x in ("here_f", "after_f", "other_f"))
        eq_f, end_f, cap_f = (sb(x, [P, T, P], F32) for x in ("eq_f", "end_f", "cap_f"))
        eq_b = sb("eq_b", [P, T, P], BF16)
        tabs_sb = (core.other_idx, core.node_idx, core.end_idx)
        heads = sb("heads", [1, HALF], I32)
        first0 = sb("first0", [1, 1], BF16)
        filled, loaded, float_ok, eq_ok, tabs, transposed, same_ok, heads_in = (core.sem(name + x) for x in (
            "filled", "loaded", "floats", "equal", "tables", "transposed", "flags", "heads_in"))
        block = s.enter_context(nc.Block())
        count = []

        @block.sync
        def _(sp):
            sp.wait_ge(filled, 4)
            count.append(16 * load(sp, here_t, after_t, other_t, loaded))
            if first_nodes is not None:
                with nc.allow_non_contiguous_dma(reason="one number of every 2 GR edges"):
                    sp.dma_start(heads[:, :], first_nodes).then_inc(heads_in, 16)
            sp.wait_ge(eq_ok, 3)
            sp.dma_start(core.same_row[0:1, 0:1], first0[:, :]).then_inc(same_ok, 16)
            sp.dma_start(core.same_row[0:1, 1:1 + NB * P * P].rearrange("a (b j p) -> (a j) b p", b=NB, p=P),
                         eq_b[:, 0:NB, :]).then_inc(same_ok, 16)
            sp.dma_start(core.same_row[0:1, 1 + NB * P * P:1 + NP].rearrange("a (j p) -> (a j) p", p=P),
                         eq_b[0:NT - NB * P, NB, :]).then_inc(same_ok, 16)
            sp.wait_ge(same_ok, 48)

        @block.vector
        def _(dve):
            nc.vector.memset(here_i, PAD_DST).then_inc(filled, 1)
            nc.vector.memset(other_i, 0).then_inc(filled, 1)
            nc.vector.memset(after_t[:, :, :, :] if paired else after_i, PAD_DST + 1).then_inc(filled, 1)
            nc.vector.memset(first0[:, :], 0.0).then_inc(filled, 1)
            dve.wait_ge(loaded, count[0])
            nc.vector.tensor_copy(here_f[:, :, :], here_i).then_inc(float_ok, 1)
            nc.vector.tensor_copy(after_f[:, :, :], after_i).then_inc(float_ok, 1)
            nc.vector.tensor_copy(other_f[:, :, :], other_i).then_inc(float_ok, 1)
            dve.wait_ge(float_ok, 3)
            nc.vector.tensor_tensor(eq_f[:, :, :], here_f[:, :, :], after_f[:, :, :], ALU.is_equal).then_inc(eq_ok, 1)
            nc.vector.tensor_scalar(cap_f[:, :, :], here_f[:, :, :], float(N - 1), None, ALU.min).then_inc(eq_ok, 1)
            dve.wait_ge(eq_ok, 2)
            nc.vector.tensor_copy(eq_b[:, :, :], eq_f[:, :, :]).then_inc(eq_ok, 1)
            nc.vector.scalar_tensor_tensor(out=end_f[:, :, :], in0=eq_f[:, :, :], scalar=float(FAR), in1=here_f[:, :, :],
                                           op0=ALU.mult, op1=ALU.add).then_inc(eq_ok, 1)
            for n in range(3):
                dve.wait_ge(transposed, n + 1)
                nc.vector.tensor_copy(tabs_sb[n][:, 0:NT], core.bank[n][:, 0:NT]).then_inc(tabs, 1)
            nc.vector.tensor_scalar(core.other_idx[:, NT:2 * NT], core.bank[0][:, 0:NT], float(NP), None, ALU.add).then_inc(tabs, 1)
            if first_nodes is not None:
                nc.vector.memset(core.nodes_done[:, :], 0).then_inc(tabs, 1)
                dve.wait_ge(heads_in, 16)
                dve.wait_ge(tabs, 5)
                nc.vector.tensor_scalar(core.nodes_done[0:1, BEHIND + 1:HALF + 1], heads[0:1, 1:HALF + 1 - BEHIND], HEAD_SHIFT, None,
                                        ALU.logical_shift_right).then_inc(tabs, 1)

        @block.tensor
        def _(pe):
            pe.wait_ge(float_ok, 3)
            for n, (tile, ready) in enumerate(((other_f, 2), (cap_f, 3), (end_f, 4))):
                pe.wait_ge(eq_ok, ready)
                for b in range(T):
                    last = nc.tensor.transpose(core.bank[n][:, b * P:(b + 1) * P], tile[:, b, :], core.ident[:, :])
                last.then_inc(transposed, 1)


def message_passing(core, x, W_edge, b_edge, W_agg, b_agg):
    nc, bank, ident = core.nc, core.bank, core.ident
    with ExitStack() as s:
        def sb(name, shape, dt=F32):
            return s.enter_context(nc.sbuf_tensor(name, shape, dt))

        def two(name, shape, dt=F32):
            return [sb(f"{name}{k}", shape, dt) for k in range(2)]
        w_edge, w_agg_a, w_agg_h = sb("mp_w_edge", [D, D]), sb("mp_w_agg_a", [D, D]), sb("mp_w_agg_h", [D, D])
        bias_edge, bias_agg = sb("mp_b_edge", [D, 1]), sb("mp_b_agg", [D, 1])
        agg_in = two("mp_agg_in", [P, GR])
        h_in, h_out = two("mp_h_in", [D, GR]), two("mp_h_out", [D, GR])
        msg_out = two("mp_msg_out", [P, GR])
        src_ix, end_ix = two("mp_src_ix", [P, T], I32), two("mp_end_ix", [P, T], I32)
        gathered = two("mp_gathered", [P, T, D])
        relu_msg, run_sum = two("mp_relu_msg", [D, GR]), two("mp_run_sum", [D, GR])
        seg_rows = two("mp_seg_rows", [P, T, D])
        FLAG_PARTS = [0, *range(4, NG, 8)]
        wts, same_in = core.sem("mp_weights_in"), [core.sem(f"mp_flags_in{k}") for k in range(2)]
        g_in = [core.sem(f"mp_gathered{k}") for k in range(2)]
        sc_out = [core.sem(f"mp_scattered{k}") for k in range(2)]
        ix_ok = core.sem("mp_index_ready")
        g_t, relu_ok, sum_ok = core.sem("mp_gather_transposed"), core.sem("mp_relu_ready"), core.sem("mp_sum_ready")
        seg_mm, seg_ok = core.sem("mp_segment_product"), core.sem("mp_segment_rows_ready")
        nd_in = [core.sem(f"mp_node_in{k}") for k in range(2)]
        h_mm, h_ok, m_mm, m_ok = (core.sem(n) for n in ("mp_h_product", "mp_h_ready", "mp_m_product", "mp_m_ready"))
        h_st, m_st = [core.sem(f"mp_h_stored{k}") for k in range(2)], [core.sem(f"mp_m_stored{k}") for k in range(2)]

        def layer_work(eng, edge, node):
            edge(0)
            edge(1)
            with eng.Fori(2, HALF) as i:
                edge(i)
                done = eng.value_load(core.nodes_done[0:1, bass.ds(i, 1)], min_val=0, max_val=HALF - 1)
                due = eng.value_load(core.nodes_done[0:1, bass.ds(i + 1, 1)], min_val=0, max_val=HALF - 1)
                with eng.If(done < due):
                    with eng.Fori(done, due) as n:
                        node(n, i + 1 - BEHIND)
            done = eng.value_load(core.nodes_done[0:1, HALF:HALF + 1], min_val=0, max_val=HALF - 1)
            with eng.Fori(done, HALF) as n:
                node(n, HALF)

        with nc.Block() as block:
            @block.sync
            def _(sp):
                with nc.allow_non_contiguous_dma(reason="one bias value per partition"):
                    sp.dma_start(w_edge[:, :], W_edge).then_inc(wts, 16)
                    sp.dma_start(w_agg_a[:, :], W_agg[0:D, :]).then_inc(wts, 16)
                    sp.dma_start(w_agg_h[:, :], W_agg[D:2 * D, :]).then_inc(wts, 16)
                    sp.dma_start(bias_edge[:, :], b_edge.rearrange("(p a) -> p a", a=1)).then_inc(wts, 16)
                    sp.dma_start(bias_agg[:, :], b_agg.rearrange("(p a) -> p a", a=1)).then_inc(wts, 16)

                for n, g in enumerate(FLAG_PARTS):
                    reached(sp, same_in[n % 2], 16 * (n // 2))
                    sp.dma_start(*core.flags(g, (FLAG_PARTS + [NG])[n + 1] - g)).then_inc(same_in[n % 2], 16)
                with sp.Fori(0, LAYERS) as layer:
                    base, turn = layer * NG, layer * HALF

                    def node(n, summed):
                        for k in range(2):
                            reached(sp, sc_out[k], 64 * summed, turn * 64)
                        for k in range(2):
                            g = 2 * n + k
                            sp.dma_start(agg_in[k][:, :], rows_of_group(core.agg_rows, g, D)).then_inc(nd_in[k], 16)
                            sp.dma_start(h_in[k][:, :], core.h_cols[:, bass.ds(g * GR, GR)]).then_inc(nd_in[k], 16)
                        for k in range(2):
                            g = 2 * n + k
                            reached(sp, h_ok, g + 1, base)
                            sp.dma_start(core.h_cols[:, bass.ds(g * GR, GR)], h_out[k][:, :]).then_inc(h_st[k], 16)
                        for k in range(2):
                            g = 2 * n + k
                            to = ((layer + 1) & 1) * NP + g * GR
                            reached(sp, m_ok, g + 1, base)
                            sp.dma_start(core.msg_rows[bass.ds(to, GR), :].rearrange("(p k) f -> p (k f)", k=T),
                                         msg_out[k][:, :]).then_inc(m_st[k], 16)
                        for k in range(2):
                            reached(sp, h_st[k], 16 * (n + 1), turn * 16)
                            reached(sp, m_st[k], 16 * (n + 1), turn * 16)
                    layer_work(sp, lambda i: None, node)

            @block.gpsimd
            def _(pool):
                with pool.Fori(0, LAYERS) as layer:
                    base, turn = layer * NG, layer * HALF

                    def gather(i, k):
                        reached(pool, g_in[k], 64 * i, turn * 64)
                        reached(pool, g_t, 2 * i + k - 1, base)
                        pool.nop(nofuse=True)
                        at = (layer & 1) * NT + (2 * i + k) * T
                        nc.gpsimd.tensor_copy(src_ix[k][:, :], core.other_idx[:, bass.ds(at, T)]).then_inc(ix_ok, 1)

                    def gather_start(i, k, step):
                        pool.wait_ge(ix_ok, 2 * base + 4 * i + step)
                        pool.nop(nofuse=True)
                        for t in range(T):
                            pool.indirect_dma_start(gathered[k][:, t, :], None, core.msg_rows,
                                                    bass.IndirectOffsetOnAxis(ap=src_ix[k][:, t:t + 1], axis=0)).then_inc(g_in[k], 16)

                    def scatter(i, k, j, step):
                        reached(pool, sc_out[k], 64 * i, turn * 64)
                        pool.nop(nofuse=True)
                        nc.gpsimd.tensor_copy(end_ix[k][:, :], core.end_idx[:, bass.ds((2 * i + k) * T, T)]).then_inc(ix_ok, 1)
                        pool.wait_ge(ix_ok, 2 * base + 4 * j + step)
                        pool.wait_ge(seg_ok, base + 2 * i + k + 1)
                        pool.nop(nofuse=True)
                        for t in range(T):
                            pool.indirect_dma_start(core.agg_rows, bass.IndirectOffsetOnAxis(ap=end_ix[k][:, t:t + 1], axis=0),
                                                    seg_rows[k][:, t, :], None, bounds_check=NP - 1, oob_is_err=False).then_inc(sc_out[k], 16)

                    def body(i):
                        for k in range(2):
                            if isinstance(i, int) and i == 0:
                                gather(0, k)
                                gather_start(0, k, k + 1)
                            else:
                                gather(i, k)
                                gather_start(i, k, 2 * k - 1)
                                scatter(i - 1, k, i, 2 * k)
                    halves(pool, body)
                    for k in range(2):
                        scatter(HALF - 1, k, HALF, k - 1)
                    for k in range(2):
                        pool.wait_ge(m_st[k], turn * 16 + 16 * HALF)
                    pool.nop(nofuse=True)

            @block.tensor
            def _(pe):
                pe.wait_ge(wts, 5 * 16)
                with pe.Fori(0, LAYERS) as layer:
                    base, turn = layer * NG, layer * HALF

                    def edge(i):
                        for k in range(2):
                            g = 2 * i + k
                            pe.wait_ge(g_in[k], turn * 64 + 64 * (i + 1))
                            reached(pe, relu_ok, g - 1, base)
                            for t in range(T):
                                last = nc.tensor.transpose(bank[k][:, t * P:(t + 1) * P], gathered[k][:, t, :], ident[:, :])
                            last.then_inc(g_t, 1)
                            pe.wait_ge(sum_ok, base + g + 1)
                            reached(pe, seg_ok, g - 1, base)
                            for t in range(T):
                                last = nc.tensor.matmul(bank[2 + k][:, t * P:(t + 1) * P], run_sum[k][:, t * P:(t + 1) * P],
                                                        w_agg_a[:, :], start=True, stop=True)
                            last.then_inc(seg_mm, 1)

                    def node(n, summed):
                        for k in range(2):
                            pe.wait_ge(nd_in[k], turn * 32 + 32 * (n + 1))
                            for t in range(T):
                                part = slice(t * P, (t + 1) * P)
                                nc.tensor.matmul(bank[4 + k][:, part], w_agg_h[:, :], h_in[k][:, part], start=True, stop=False)
                                last = nc.tensor.matmul(bank[4 + k][:, part], agg_in[k][:, part], ident[:, :], start=False, stop=True)
                            last.then_inc(h_mm, 1)
                        for k in range(2):
                            pe.wait_ge(h_ok, base + 2 * n + k + 1)
                            for t in range(T):
                                last = nc.tensor.matmul(bank[6 + k][:, t * P:(t + 1) * P], h_out[k][:, t * P:(t + 1) * P], w_edge[:, :],
                                                        start=True, stop=True)
                            last.then_inc(m_mm, 1)
                    layer_work(pe, edge, node)

            @block.scalar
            def _(act):
                act.wait_ge(wts, 5 * 16)
                with act.Fori(0, LAYERS) as layer:
                    base, turn = layer * NG, layer * HALF

                    def edge(i):
                        for k in range(2):
                            g = 2 * i + k
                            act.wait_ge(g_t, base + g + 1)
                            reached(act, sum_ok, g - 1, base)
                            nc.scalar.activation(relu_msg[k][:, :], bank[k][:, :], ACT.Relu, bias=bias_edge[:, 0:1]).then_inc(relu_ok, 1)
                            act.wait_ge(seg_mm, base + g + 1)
                            reached(act, sc_out[k], 64 * i, turn * 64)
                            nc.scalar.activation(seg_rows[k][:, :, :], bank[2 + k][:, :], ACT.Copy).then_inc(seg_ok, 1)

                    def node(n, summed):
                        for k in range(2):
                            act.wait_ge(h_mm, base + 2 * n + k + 1)
                            nc.scalar.activation(h_out[k][:, :], bank[4 + k][:, :], ACT.Relu, bias=bias_agg[:, 0:1]).then_inc(h_ok, 1)
                    layer_work(act, edge, node)

            @block.vector
            def _(dve):
                with dve.Fori(0, LAYERS) as layer:
                    base, turn = layer * NG, layer * HALF

                    def edge(i):
                        for k in range(2):
                            g = 2 * i + k
                            start = 0.0 if isinstance(g, int) and g == 0 else run_sum[1 - k][:, GR - 1:GR]
                            if isinstance(i, int):
                                dve.wait_ge(same_in[0], 16)
                            else:
                                for n in range(2):
                                    dve.wait_ge(same_in[n], 16 * ((len(FLAG_PARTS) + 1 - n) // 2))
                            dve.wait_ge(relu_ok, base + g + 1)
                            reached(dve, seg_mm, g - 1, base)
                            reached(dve, sum_ok, g, base)
                            nc.vector.tensor_tensor_scan(run_sum[k][:, :], core.same[:, bass.ds(g * GR, GR)], relu_msg[k][:, :],
                                                         start, ALU.mult, ALU.add).then_inc(sum_ok, 1)

                    def node(n, summed):
                        for k in range(2):
                            dve.wait_ge(m_mm, base + 2 * n + k + 1)
                            nc.vector.tensor_copy(msg_out[k][:, :], bank[6 + k][:, :]).then_inc(m_ok, 1)
                    layer_work(dve, edge, node)


def norm_stats(nc, dve, chain, at, rows, stats, moments):
    for t in range(T):
        last = nc.vector.bn_stats(stats[:, t, :], rows[:, t, :])
    last.then_inc(chain, 1)
    dve.wait_ge(chain, at + 1)
    dve.nop(nofuse=True)
    for t in range(T):
        last = nc.vector.bn_aggr(moments[:, t, :], stats[:, t, :])
    return last


def inverse_deviation(nc, pool, chain, at, moments, eps_var, half, out):
    pool.nop(nofuse=True)
    nc.gpsimd.tensor_scalar(eps_var[:, :], moments[:, :, 1], EPS, None, ALU.add).then_inc(chain, 1)
    pool.wait_ge(chain, at + 1)
    return nc.gpsimd.tensor_tensor(out[:, :], eps_var[:, :], half[:, :], ALU.pow)


def project_nodes(core, x, w, b):
    nc, bank, ident = core.nc, core.bank, core.ident
    NPJ = 4 * D
    with ExitStack() as s:
        def sb(name, shape, dt=F32):
            return s.enter_context(nc.sbuf_tensor(name, shape, dt))

        def two(name, shape, dt=F32):
            return [sb(f"{name}{k}", shape, dt) for k in range(2)]
        weights, bias = sb("pn_weights", [D, NPJ]), sb("pn_bias", [P, NPJ])
        x_in, h_in = two("pn_x_in", [P, T, D]), two("pn_h_in", [D, GR])
        y = two("pn_y", [P, T, D])
        stats, moments = two("pn_stats", [P, T, 6]), two("pn_moments", [P, T, 2])
        half, eps_var, rstd = sb("pn_half", [P, T]), two("pn_eps_var", [P, T]), two("pn_rstd", [P, T])
        x1, x1_bias, x1_cols = two("pn_x1", [P, T, D]), two("pn_x1_bias", [P, T, D]), two("pn_x1_cols", [D, GR])
        proj = two("pn_proj", [P, T, NPJ])
        h_bank, x1_bank, proj_bank = bank[0:2], bank[2:4], bank[4:8]
        wts, half_ok, same_in = core.sem("pn_weights_in"), core.sem("pn_half_ready"), core.sem("pn_flags_in")
        ld = [core.sem(f"pn_in{k}") for k in range(2)]
        h_t, y_ok, stat_c, mom_ok, pow_c, rstd_ok, x1_ok, xb_ok = (core.sem("pn_" + n) for n in (
            "h_transposed", "y_ready", "stats_chain", "moments_ready", "pow_chain", "rstd_ready", "x1_ready", "x1_bias_ready"))
        x1_t, cols_ok, mm, pr_ok = (core.sem("pn_" + n) for n in ("x1_transposed", "x1_cols_ready", "product", "proj_ready"))
        st_x1, st = ([core.sem(f"pn_{n}{k}") for k in range(2)] for n in ("x1_stored", "proj_stored"))
        block = s.enter_context(nc.Block())

        def rows(t, g):
            return t[bass.ds(g * GR, GR), :].rearrange("(p k) f -> p k f", k=T)

        @block.sync
        def _(sp):
            for n, name in enumerate(("Wk", "Wv", "Wq", "Wskip")):
                sp.dma_start(weights[:, n * D:(n + 1) * D], w[name]).then_inc(wts, 16)
            for n, name in enumerate(("bk", "bv", "bq", "bskip")):
                sp.dma_start(bias[:, n * D:(n + 1) * D], b[name].partition_broadcast(P)).then_inc(wts, 16)

            def load(g, k, i):
                reached(sp, y_ok, g - 1)
                if isinstance(g, int) and g == NG - 1:
                    sp.dma_start(x_in[k][0:LAST, :, :], x[g * GR:N, :].rearrange("(p k) f -> p k f", k=T)).then_inc(ld[k], 16)
                else:
                    sp.dma_start(x_in[k][:, :, :], rows(x, g)).then_inc(ld[k], 16)
                sp.dma_start(h_in[k][:, :], core.h_cols[:, bass.ds(g * GR, GR)]).then_inc(ld[k], 16)

            def spread_flags(g, k, i):
                sp.dma_start(*core.flags(g, 1)).then_inc(same_in, 16)

            def store_x1(g, k, i):
                reached(sp, x1_ok, g + 1)
                sp.dma_start(rows(core.x1_rows, g), x1[k][:, :, :]).then_inc(st_x1[k], 16)

            def store(g, k, i):
                sp.wait_ge(pr_ok, T * (g + 1))
                sp.nop(nofuse=True)
                sp.dma_start(rows(core.kv_rows, g), proj[k][:, :, 0:2 * D]).then_inc(st[k], 16)
                sp.dma_start(rows(core.q_rows, g), proj[k][:, :, 2 * D:3 * D]).then_inc(st[k], 16)
                sp.dma_start(rows(core.skip_rows, g), proj[k][:, :, 3 * D:4 * D]).then_inc(st[k], 16)

            def turn(do):
                do(0, store_x1)
                do(3, load)
                do(0, spread_flags)
                do(-1, store)
            turns(sp, turn)
            sp.wait_ge(same_in, 16 * NG)
            for k in range(2):
                sp.wait_ge(st_x1[k], 16 * HALF)
                sp.wait_ge(st[k], 48 * HALF)

        @block.tensor
        def _(pe):
            pe.wait_ge(wts, 8 * 16)

            def turn_h(g, k, i):
                pe.wait_ge(ld[k], 32 * (i + 1))
                reached(pe, y_ok, g - 1)
                for t in range(T):
                    last = nc.tensor.transpose(h_bank[k][:, t * P:(t + 1) * P], h_in[k][:, t * P:(t + 1) * P], ident[:, :])
                last.then_inc(h_t, 1)

            def turn_x1(g, k, i):
                pe.wait_ge(x1_ok, g + 1)
                reached(pe, cols_ok, g - 1)
                for t in range(T):
                    last = nc.tensor.transpose(x1_bank[k][:, t * P:(t + 1) * P], x1[k][:, t, :], ident[:, :])
                last.then_inc(x1_t, 1)

            def project(g, k, i):
                pe.wait_ge(cols_ok, g + 1)
                for t in range(T):
                    reached(pe, pr_ok, T * (g - 1) + t + 1)
                    nc.tensor.matmul(proj_bank[t][:, :], x1_cols[k][:, t * P:(t + 1) * P], weights[:, :],
                                     start=True, stop=True).then_inc(mm, 1)

            def turn(do):
                do(2, turn_h)
                do(0, turn_x1)
                do(-1, project)
            turns(pe, turn)

        @block.scalar
        def _(act):
            def x1_columns(g, k, i):
                act.wait_ge(x1_t, g + 1)
                reached(act, mm, T * (g - 1))
                nc.scalar.activation(x1_cols[k][:, :], x1_bank[k][:, :], ACT.Copy).then_inc(cols_ok, 1)

            def turn(do):
                do(0, x1_columns)
            turns(act, turn)

        @block.gpsimd
        def _(pool):
            nc.gpsimd.memset(half[:, :], -0.5).then_inc(half_ok, 1)
            pool.wait_ge(half_ok, 1)
            pool.wait_ge(wts, 8 * 16)

            def power(g, k, i):
                pool.wait_ge(mom_ok, g + 1)
                reached(pool, x1_ok, g - 1)
                inverse_deviation(nc, pool, pow_c, g, moments[k], eps_var[k], half, rstd[k]).then_inc(rstd_ok, 1)

            def add_bias(g, k, i):
                pool.wait_ge(x1_ok, g + 1)
                reached(pool, pr_ok, T * (g - 1))
                nc.gpsimd.tensor_tensor(x1_bias[k][:, :, :], x1[k][:, :, :],
                                        bias[:, 3 * D:4 * D].unsqueeze(1).broadcast_to([P, T, D]), ALU.add).then_inc(xb_ok, 1)

            def turn(do):
                do(0, add_bias)
                do(1, power)
            turns(pool, turn)

        @block.vector
        def _(dve):
            dve.wait_ge(wts, 8 * 16)

            def add_h(g, k, i):
                dve.wait_ge(h_t, g + 1)
                dve.wait_ge(ld[k], 32 * (i + 1))
                reached(dve, x1_ok, g - 1)
                nc.vector.tensor_tensor(y[k][:, :, :], h_bank[k][:, :].rearrange("p (t f) -> p t f", t=T), x_in[k][:, :, :], ALU.add).then_inc(y_ok, 1)
                dve.wait_ge(y_ok, g + 1)
                reached(dve, rstd_ok, g - 1)
                norm_stats(nc, dve, stat_c, g, y[k], stats[k], moments[k]).then_inc(mom_ok, 1)

            def normalize(g, k, i):
                dve.wait_ge(mom_ok, g + 1)
                dve.wait_ge(rstd_ok, g + 1)
                reached(dve, xb_ok, g - 1)
                reached(dve, x1_t, g - 1)
                reached(dve, st_x1[k], 16 * i)
                for t in range(T):
                    last = nc.vector.tensor_scalar(x1[k][:, t, :], y[k][:, t, :], moments[k][:, t, 0:1], rstd[k][:, t:t + 1],
                                                   ALU.subtract, ALU.mult)
                last.then_inc(x1_ok, 1)

            def add_biases(g, k, i):
                reached(dve, st[k], 48 * i)
                for t in range(T):
                    dve.wait_ge(mm, T * g + t + 1)
                    nc.vector.tensor_tensor(proj[k][:, t, 0:3 * D], proj_bank[t][:, 0:3 * D], bias[:, 0:3 * D], ALU.add)
                    if t == 0:
                        dve.wait_ge(xb_ok, g + 1)
                    nc.vector.tensor_tensor(proj[k][:, t, 3 * D:4 * D], proj_bank[t][:, 3 * D:4 * D], x1_bias[k][:, t, :], ALU.add).then_inc(pr_ok, 1)

            def turn(do):
                do(0, normalize)
                do(1, add_h)
                do(-1, add_biases)
            turns(dve, turn)


def attention(core, edge_attr, We):
    nc, bank, ident = core.nc, core.bank, core.ident
    with ExitStack() as s:
        def sb(name, shape, dt=F32):
            return s.enter_context(nc.sbuf_tensor(name, shape, dt))

        def two(name, shape, dt=F32):
            return [sb(f"{name}{k}", shape, dt) for k in range(2)]
        w_e, expand = sb("at_we", [ED, D]), sb("at_expand", [H, D])
        src_ix, dst_ix, end_ix = (two(f"at_{n}_ix", [P, T], I32) for n in ("src", "dst", "end"))
        kv, q = two("at_kv", [P, T, 2 * D]), two("at_q", [P, T, D])
        attr, attr_cols = two("at_attr", [P, T, ED]), sb("at_attr_cols", [ED, GR])
        k_e, v_e, prod = sb("at_k_e", [P, T, D]), two("at_v_e", [P, T, D]), sb("at_prod", [P, T, D])
        logits = two("at_logits", [P, T, H])
        logit_c, brk = two("at_logit_cols", [H, GR]), two("at_break", [H, GR])
        top = two("at_top", [H, 1 + GR])
        drop, decay, weight = sb("at_drop", [H, GR]), two("at_decay", [H, GR]), two("at_weight", [H, GR])
        decay_d, wv = sb("at_decay_rows", [D, GR]), sb("at_weighted", [P, T, D])
        num, den = two("at_num", [D, GR]), two("at_den", [H, GR])
        inv, rows = sb("at_inv", [P, T * H]), two("at_rows", [P, T, D])
        attr_bank, e_bank, logit_bank, weight_bank, decay_bank, wv_bank, num_bank, den_bank = bank
        wts, setup, rest_in = core.sem("at_weights_in"), core.sem("at_setup"), core.sem("at_rest_in")
        ix_ok, end_ok = core.sem("at_index_ready"), core.sem("at_end_index_ready")
        g_in, a_in, sc_out = ([core.sem(f"at_{n}{k}") for k in range(2)] for n in ("gathered", "attr_in", "scattered"))
        (a_t, a_ok, e_mm, ve_ok, ke_ok, prod_ok, log_ok, log_t, logc_ok, brk_ok, top_ok, drop_ok, diff_ok, w_ok, dec_ok) = (
            core.sem("at_" + n) for n in (
                "attr_transposed", "attr_cols_ready", "e_product", "v_e_ready", "k_e_ready", "prod_ready", "logits_ready",
                "logits_transposed", "logit_cols_ready", "break_ready", "top_ready", "drop_ready", "differences_ready",
                "weight_ready", "decay_ready"))
        w_t, dec_mm, decd_ok, wv_ok, wv_t, den_ok, num_ok, back_t, cap_ok, inv_ok, rows_ok = (
            core.sem("at_" + n) for n in (
                "weight_transposed", "decay_product", "decay_rows_ready", "weighted_ready", "weighted_transposed", "den_ready",
                "num_ready", "sums_transposed", "den_guarded", "inverse_ready", "rows_ready"))
        block = s.enter_context(nc.Block())

        @block.sync
        def _(sp):
            sp.dma_start(w_e[:, :], We).then_inc(wts, 16)
            sp.wait_ge(setup, 3)

            def load(g, k, i):
                reached(sp, a_t, g - 1)
                if isinstance(g, int) and g == NG - 1:
                    whole, rest = (E - g * GR) // P, (E - g * GR) % P
                    sp.dma_start(attr[k][0:rest, whole, :], edge_attr[g * GR + whole * P:E, :]).then_inc(rest_in, 16)
                    sp.wait_ge(rest_in, 16)
                    sp.dma_start(attr[k][:, 0:whole, :], edge_attr[g * GR:g * GR + whole * P, :].rearrange("(t p) f -> p t f", p=P)).then_inc(a_in[k], 16)
                else:
                    sp.dma_start(attr[k][:, :, :], edge_attr[bass.ds(g * GR, GR), :].rearrange("(t p) f -> p t f", p=P)).then_inc(a_in[k], 16)

            def turn(do):
                do(3, load)
            turns(sp, turn)
            for k in range(2):
                sp.wait_ge(sc_out[k], 64 * HALF)

        @block.gpsimd
        def _(pool):
            pool.memset(expand[:, :], 1.0).then_inc(setup, 1)
            pool.wait_ge(setup, 3)
            pool.affine_select(out=expand[:, :], in_=expand[:, :], compare_op=ALU.is_ge, fill=0.0,
                               base=0, pattern=[[1, D]], channel_multiplier=-C).then_inc(setup, 1)
            pool.wait_ge(setup, 4)
            pool.affine_select(out=expand[:, :], in_=expand[:, :], compare_op=ALU.is_ge, fill=0.0,
                               base=C - 1, pattern=[[-1, D]], channel_multiplier=C).then_inc(setup, 1)

            def gather(g, k, i):
                reached(pool, prod_ok, g - 1)
                pool.nop(nofuse=True)
                nc.gpsimd.tensor_copy(src_ix[k][:, :], core.other_idx[:, bass.ds(g * T, T)]).then_inc(ix_ok, 1)
                nc.gpsimd.tensor_copy(dst_ix[k][:, :], core.node_idx[:, bass.ds(g * T, T)]).then_inc(ix_ok, 1)
                pool.wait_ge(ix_ok, 2 * g + 2)
                pool.nop(nofuse=True)
                for t in range(T):
                    pool.indirect_dma_start(kv[k][:, t, :], None, core.kv_rows,
                                            bass.IndirectOffsetOnAxis(ap=src_ix[k][:, t:t + 1], axis=0)).then_inc(g_in[k], 16)
                    pool.indirect_dma_start(q[k][:, t, :], None, core.q_rows,
                                            bass.IndirectOffsetOnAxis(ap=dst_ix[k][:, t:t + 1], axis=0)).then_inc(g_in[k], 16)

            def scatter(g, k, i):
                reached(pool, sc_out[k], 64 * i)
                pool.nop(nofuse=True)
                nc.gpsimd.tensor_copy(end_ix[k][:, :], core.end_idx[:, bass.ds(g * T, T)]).then_inc(end_ok, 1)
                pool.wait_ge(end_ok, g + 1)
                pool.wait_ge(rows_ok, g + 1)
                pool.nop(nofuse=True)
                for t in range(T):
                    pool.indirect_dma_start(core.conv_rows, bass.IndirectOffsetOnAxis(ap=end_ix[k][:, t:t + 1], axis=0),
                                            rows[k][:, t, :], None, bounds_check=NP - 1, oob_is_err=False).then_inc(sc_out[k], 16)

            def turn(do):
                do(1, gather)
                do(-4, scatter)
            turns(pool, turn)

        @block.tensor
        def _(pe):
            pe.wait_ge(wts, 16)
            pe.wait_ge(setup, 5)

            def turn_weight(g, k, i):
                pe.wait_ge(w_ok, g + 1)
                reached(pe, wv_ok, g)
                pe.nop(nofuse=True)
                for t in range(T):
                    last = nc.tensor.transpose(weight_bank[:, t * H:(t + 1) * H], weight[k][:, t * P:(t + 1) * P], ident[0:H, 0:H])
                last.then_inc(w_t, 1)

            def expand_decay(g, k, i):
                pe.wait_ge(dec_ok, g + 1)
                reached(pe, decd_ok, g)
                pe.nop(nofuse=True)
                nc.tensor.matmul(decay_bank[:, :], expand[:, :], decay[k][:, :], start=True, stop=True).then_inc(dec_mm, 1)

            def turn_back(g, k, i):
                pe.wait_ge(num_ok, g + 1)
                pe.wait_ge(den_ok, g + 1)
                reached(pe, rows_ok, g)
                for t in range(T):
                    nc.tensor.transpose(num_bank[:, t * P:(t + 1) * P], num[k][:, t * P:(t + 1) * P], ident[:, :])
                for t in range(T):
                    last = nc.tensor.transpose(den_bank[:, t * H:(t + 1) * H], den[k][:, t * P:(t + 1) * P], ident[0:H, 0:H])
                last.then_inc(back_t, 1)

            def turn_weighted(g, k, i):
                pe.wait_ge(wv_ok, g + 1)
                reached(pe, num_ok, g)
                for t in range(T):
                    last = nc.tensor.transpose(wv_bank[:, t * P:(t + 1) * P], wv[:, t, :], ident[:, :])
                last.then_inc(wv_t, 1)

            def turn_logits(g, k, i):
                pe.wait_ge(log_ok, g + 1)
                reached(pe, logc_ok, g)
                for t in range(T):
                    last = nc.tensor.transpose(logit_bank[0:H, t * P:(t + 1) * P], logits[k][:, t, :], ident[:, :])
                last.then_inc(log_t, 1)

            def edge_features(g, k, i):
                pe.wait_ge(a_in[k], 16 * (i + 1))
                reached(pe, a_ok, g)
                pe.nop(nofuse=True)
                for t in range(T):
                    last = nc.tensor.transpose(attr_bank[0:ED, t * P:(t + 1) * P], attr[k][:, t, :], ident[:, :])
                last.then_inc(a_t, 1)
                pe.wait_ge(a_ok, g + 1)
                reached(pe, ke_ok, g)
                for t in range(T):
                    last = nc.tensor.matmul(e_bank[:, t * P:(t + 1) * P], attr_cols[:, t * P:(t + 1) * P], w_e[:, :],
                                            start=True, stop=True)
                last.then_inc(e_mm, 1)

            def turn(do):
                do(-2, turn_weight)
                do(-2, expand_decay)
                do(-3, turn_back)
                do(-2, turn_weighted)
                do(0, turn_logits)
                do(1, edge_features)
            turns(pe, turn)

        @block.scalar
        def _(act):
            def decay_copy(g, k, i):
                act.wait_ge(dec_mm, g + 1)
                reached(act, num_ok, g)
                nc.scalar.activation(decay_d[:, :], decay_bank[:, :], ACT.Copy).then_inc(decd_ok, 1)

            def breaks(g, k, i):
                reached(act, drop_ok, g - 1)
                nc.scalar.activation(brk[k][:, :], core.same[0:H, bass.ds(g * GR, GR)], ACT.Copy, scale=BIG, bias=-BIG).then_inc(brk_ok, 1)

            def logit_copy(g, k, i):
                act.wait_ge(log_t, g + 1)
                reached(act, diff_ok, 2 * (g - 1))
                nc.scalar.activation(logit_c[k][:, :], logit_bank[0:H, :], ACT.Copy, scale=float(C) ** -0.5).then_inc(logc_ok, 1)

            def attr_copy(g, k, i):
                act.wait_ge(a_t, g + 1)
                reached(act, e_mm, g)
                nc.scalar.activation(attr_cols[:, :], attr_bank[0:ED, :], ACT.Copy).then_inc(a_ok, 1)

            def exponentials(g, k, i):
                act.wait_ge(diff_ok, 2 * g + 2)
                nc.scalar.activation(weight[k][:, :], weight[k][:, :], ACT.Exp).then_inc(w_ok, 1)
                nc.scalar.activation(decay[k][:, :], decay[k][:, :], ACT.Exp).then_inc(dec_ok, 1)

            def turn(do):
                do(-2, decay_copy)
                do(0, breaks)
                do(0, logit_copy)
                do(1, attr_copy)
                do(-1, exponentials)
            turns(act, turn)

        @block.vector
        def _(dve):
            for k in range(2):
                nc.vector.memset(attr[k][:, :, :], 0.0).then_inc(setup, 1)
            nc.vector.memset(top[0][:, 0:1], 0.0).then_inc(top_ok, 1)

            def weigh(g, k, i):
                dve.wait_ge(w_t, g + 1)
                dve.wait_ge(ve_ok, g + 1)
                reached(dve, wv_t, g)
                nc.vector.tensor_tensor(wv[:, :, :].rearrange("p t (h c) -> p (t h) c", h=H),
                                        v_e[k][:, :, :].rearrange("p t (h c) -> p (t h) c", h=H),
                                        weight_bank[:, 0:T * H].unsqueeze(2).broadcast_to([P, T * H, C]), ALU.mult).then_inc(wv_ok, 1)

            def den_scan(g, k, i):
                first = isinstance(g, int) and g == 0
                dve.wait_ge(w_ok, g + 1)
                dve.wait_ge(dec_ok, g + 1)
                reached(dve, back_t, g - 1)
                reached(dve, den_ok, g)
                nc.vector.tensor_tensor_scan(den[k][:, :], decay[k][:, :], weight[k][:, :],
                                             0.0 if first else den[1 - k][:, GR - 1:GR], ALU.mult, ALU.add).then_inc(den_ok, 1)

            def num_scan(g, k, i):
                first = isinstance(g, int) and g == 0
                dve.wait_ge(wv_t, g + 1)
                dve.wait_ge(decd_ok, g + 1)
                reached(dve, back_t, g - 1)
                reached(dve, num_ok, g)
                nc.vector.tensor_tensor_scan(num[k][:, :], decay_d[:, :], wv_bank[:, :],
                                             0.0 if first else num[1 - k][:, GR - 1:GR], ALU.mult, ALU.add).then_inc(num_ok, 1)

            def edge_logits(g, k, i):
                def part(a):
                    return kv[k][:, :, a * D:(a + 1) * D], e_bank[:, :].rearrange("p (t f) -> p t f", t=T)
                dve.wait_ge(g_in[k], 128 * (i + 1))
                dve.wait_ge(e_mm, g + 1)
                reached(dve, wv_ok, g - 1)
                nc.vector.tensor_tensor(v_e[k][:, :, :], *part(1), ALU.add).then_inc(ve_ok, 1)
                nc.vector.tensor_tensor(k_e[:, :, :], *part(0), ALU.add).then_inc(ke_ok, 1)
                dve.wait_ge(ke_ok, g + 1)
                dve.wait_ge(ve_ok, g + 1)
                reached(dve, log_ok, g)
                nc.vector.tensor_tensor(prod[:, :, :], q[k][:, :, :], k_e[:, :, :], ALU.mult).then_inc(prod_ok, 1)
                dve.wait_ge(prod_ok, g + 1)
                reached(dve, log_t, g - 1)
                nc.vector.tensor_reduce(logits[k][:, :, :].rearrange("p t h -> p (t h)"),
                                        prod[:, :, :].rearrange("p t (h c) -> p (t h) c", h=H), AXX, ALU.add).then_inc(log_ok, 1)

            def maxima(g, k, i):
                dve.wait_ge(logc_ok, g + 1)
                dve.wait_ge(brk_ok, g + 1)
                dve.wait_ge(top_ok, 2 * g + 1)
                nc.vector.tensor_tensor_scan(top[k][:, 1:1 + GR], brk[k][:, :], logit_c[k][:, :], top[k][:, 0:1],
                                             ALU.add, ALU.max).then_inc(top_ok, 1)
                dve.wait_ge(top_ok, 2 * g + 2)
                nc.vector.tensor_tensor(drop[:, :], top[k][:, 0:GR], brk[k][:, :], ALU.add).then_inc(drop_ok, 1)
                reached(dve, w_t, g - 1)
                nc.vector.tensor_tensor(weight[k][:, :], logit_c[k][:, :], top[k][:, 1:1 + GR], ALU.subtract).then_inc(diff_ok, 1)
                nc.vector.tensor_copy(top[1 - k][:, 0:1], top[k][:, GR:GR + 1]).then_inc(top_ok, 1)
                dve.wait_ge(drop_ok, g + 1)
                reached(dve, dec_mm, g - 1)
                nc.vector.tensor_tensor(decay[k][:, :], drop[:, :], top[k][:, 1:1 + GR], ALU.subtract).then_inc(diff_ok, 1)

            def divide(g, k, i):
                dve.wait_ge(back_t, g + 1)
                nc.vector.tensor_scalar(inv[:, :], den_bank[:, 0:T * H], 1e-30, None, ALU.max).then_inc(cap_ok, 1)
                dve.wait_ge(cap_ok, g + 1)
                nc.vector.reciprocal(inv[:, :], inv[:, :]).then_inc(inv_ok, 1)
                dve.wait_ge(inv_ok, g + 1)
                reached(dve, sc_out[k], 64 * i)
                nc.vector.tensor_tensor(rows[k][:, :, :].rearrange("p t (h c) -> p (t h) c", h=H),
                                        num_bank[:, :].rearrange("p (n c) -> p n c", c=C),
                                        inv[:, :].unsqueeze(2).broadcast_to([P, T * H, C]), ALU.mult).then_inc(rows_ok, 1)

            def turn(do):
                do(-2, weigh)
                do(-2, den_scan)
                do(0, edge_logits)
                do(-2, num_scan)
                do(-3, divide)
                do(-1, maxima)
            turns(dve, turn)


def feed_forward(core, w, out):
    nc, bank, ident = core.nc, core.bank, core.ident
    FC = F // P
    with ExitStack() as s:
        def sb(name, shape, dt=F32):
            return s.enter_context(nc.sbuf_tensor(name, shape, dt))

        def two(name, shape, dt=F32):
            return [sb(f"{name}{k}", shape, dt) for k in range(2)]
        w1, w2 = sb("ff_w1", [D, F]), sb("ff_w2", [P, FC, D])
        g1, b1, bf1, bf2 = sb("ff_g1", [D, 1]), sb("ff_b1", [D, 1]), sb("ff_bf1", [P, FC]), sb("ff_bf2", [D, 1])
        g2, b2 = sb("ff_g2", [P, D]), sb("ff_b2", [P, D])
        agg, skip, x1 = two("ff_agg", [P, T, D]), two("ff_skip", [P, T, D]), two("ff_x1", [P, T, D])
        y, xh, h_c = two("ff_y", [P, T, D]), two("ff_xhat", [P, T, D]), two("ff_h_cols", [D, GR])
        act_c = [sb(f"ff_gelu{c}", [P, GR]) for c in range(FC)]
        hid_bank, out_bank, z_bank = (bank[1], bank[2], bank[5], bank[1]), bank[3:5], bank[6:8]
        z_c, dev = two("ff_z_cols", [D, GR]), two("ff_deviation", [P, T, D])
        x1_b2, v, fin = two("ff_x1_b2", [P, T, D]), two("ff_v", [P, T, D]), two("ff_out", [P, T, D])
        stats = [two(f"ff_stats{n}_", [P, T, 6]) for n in range(3)]
        mom = [two(f"ff_moments{n}_", [P, T, 2]) for n in range(3)]
        epv = [two(f"ff_eps_var{n}_", [P, T]) for n in range(3)]
        rstd = [two(f"ff_rstd{n}_", [P, T]) for n in range(3)]
        half, shift = sb("ff_half", [P, T]), [two(f"ff_shift{n}_", [P, T]) for n in range(3)]
        wts, half_ok = core.sem("ff_weights_in"), core.sem("ff_half_ready")
        y_in, x1_in, st = ([core.sem(f"ff_{n}{k}") for k in range(2)] for n in ("y_parts_in", "x1_in", "stored"))
        names = ("y_ready", "xhat_ready", "xhat_transposed", "h_cols_ready", "hidden_product", "gelu_ready", "out_product",
                 "z_cols_ready", "z_transposed", "deviation_ready", "x1_b2_ready", "v_ready", "out_ready")
        y_ok, xh_ok, xh_t, h_ok, f1, ge, f2, z_ok, z_t, dev_ok, xb_ok, v_ok, fin_ok = (core.sem("ff_" + n) for n in names)
        mom_ok, stat_c, pow_c, rstd_ok, shift_ok = ([core.sem(f"ff_{n}{m}") for m in range(3)] for n in (
            "moments_ready", "stats_chain", "pow_chain", "rstd_ready", "shift_ready"))
        block = s.enter_context(nc.Block())

        @block.sync
        def _(sp):
            with nc.allow_non_contiguous_dma(reason="bias values, one per partition"):
                sp.dma_start(w1[:, :], w["Wf1"]).then_inc(wts, 16)
                sp.dma_start(w2[:, :, :], w["Wf2"].rearrange("(c p) f -> p c f", p=P)).then_inc(wts, 16)
                for tile, name in ((g1, "g1"), (b1, "b1"), (bf2, "bf2")):
                    sp.dma_start(tile[:, :], w[name].rearrange("(p a) -> p a", a=1)).then_inc(wts, 16)
                sp.dma_start(bf1[:, :], w["bf1"].rearrange("(c p) -> p c", p=P)).then_inc(wts, 16)
                sp.dma_start(g2[:, :], w["g2"].partition_broadcast(P)).then_inc(wts, 16)
                sp.dma_start(b2[:, :], w["b2"].partition_broadcast(P)).then_inc(wts, 16)

            def rows(t, g):
                return t[bass.ds(g * GR, GR), :].rearrange("(p k) f -> p k f", k=T)

            def load_y(g, k, i):
                reached(sp, y_ok, g - 1)
                sp.dma_start(agg[k][:, :, :], rows(core.conv_rows, g)).then_inc(y_in[k], 16)
                sp.dma_start(skip[k][:, :, :], rows(core.skip_rows, g)).then_inc(y_in[k], 16)

            def load_x1(g, k, i):
                reached(sp, xb_ok, g - 1)
                sp.dma_start(x1[k][:, :, :], rows(core.x1_rows, g)).then_inc(x1_in[k], 16)

            def store(g, k, i):
                reached(sp, fin_ok, g + 1)
                if isinstance(g, int) and g == NG - 1:
                    sp.dma_start(out[g * GR:N, :].rearrange("(p k) f -> p k f", k=T), fin[k][0:LAST, :, :]).then_inc(st[k], 16)
                else:
                    sp.dma_start(rows(out, g), fin[k][:, :, :]).then_inc(st[k], 16)

            def turn(do):
                do(4, load_y)
                do(0, load_x1)
                do(-4, store)
            turns(sp, turn)
            for k in range(2):
                sp.wait_ge(st[k], 16 * HALF)

        @block.gpsimd
        def _(pool):
            nc.gpsimd.memset(half[:, :], -0.5).then_inc(half_ok, 1)
            pool.wait_ge(half_ok, 1)
            pool.wait_ge(wts, 8 * 16)

            def add_y(g, k, i):
                pool.wait_ge(y_in[k], 32 * (i + 1))
                reached(pool, xh_ok, g - 1)
                nc.gpsimd.tensor_tensor(y[k][:, :, :], agg[k][:, :, :], skip[k][:, :, :], ALU.add).then_inc(y_ok, 1)

            def add_b2(g, k, i):
                pool.wait_ge(x1_in[k], 16 * (i + 1))
                reached(pool, v_ok, g - 1)
                nc.gpsimd.tensor_tensor(x1_b2[k][:, :, :], x1[k][:, :, :], b2[:, :].unsqueeze(1).broadcast_to([P, T, D]), ALU.add).then_inc(xb_ok, 1)

            def power(m, used):
                def step(g, k, i):
                    pool.wait_ge(mom_ok[m], g + 1)
                    reached(pool, used, g - 1)
                    inverse_deviation(nc, pool, pow_c[m], g, mom[m][k], epv[m][k], half, rstd[m][k]).then_inc(rstd_ok[m], 1)
                return step

            def turn(do):
                do(3, add_y)
                do(-2, power(2, fin_ok))
                do(-1, add_b2)
                do(2, power(0, xh_ok))
                do(-1, power(1, v_ok))
            turns(pool, turn)

        @block.vector
        def _(dve):
            dve.wait_ge(wts, 8 * 16)

            def mean_shift(m, used):
                def step(g, k, i):
                    dve.wait_ge(mom_ok[m], g + 1)
                    dve.wait_ge(rstd_ok[m], g + 1)
                    reached(dve, used, g - 1)
                    dve.nop(nofuse=True)
                    nc.vector.scalar_tensor_tensor(out=shift[m][k][:, :], in0=mom[m][k][:, :, 0], scalar=-1.0, in1=rstd[m][k][:, :],
                                                   op0=ALU.mult, op1=ALU.mult).then_inc(shift_ok[m], 1)
                return step

            def y_moments(g, k, i):
                dve.wait_ge(y_ok, g + 1)
                reached(dve, rstd_ok[0], g - 1)
                norm_stats(nc, dve, stat_c[0], g, y[k], stats[0][k], mom[0][k]).then_inc(mom_ok[0], 1)

            def residual(g, k, i):
                dve.wait_ge(f2, g + 1)
                dve.wait_ge(h_ok, g + 1)
                reached(dve, z_t, g - 1)
                nc.vector.scalar_tensor_tensor(out=z_c[k][:, :], in0=out_bank[k][:, :], scalar=bf2[:, 0:1], in1=h_c[k][:, :],
                                               op0=ALU.add, op1=ALU.add).then_inc(z_ok, 1)

            def z_deviation(g, k, i):
                z_rows = z_bank[k][:, :].rearrange("p (t f) -> p t f", t=T)
                dve.wait_ge(z_t, g + 1)
                reached(dve, rstd_ok[1], g - 1)
                norm_stats(nc, dve, stat_c[1], g, z_rows, stats[1][k], mom[1][k]).then_inc(mom_ok[1], 1)
                dve.wait_ge(mom_ok[1], g + 1)
                reached(dve, v_ok, g - 1)
                for t in range(T):
                    last = nc.vector.scalar_tensor_tensor(out=dev[k][:, t, :], in0=z_rows[:, t, :], scalar=mom[1][k][:, t, 0:1],
                                                          in1=g2[:, :], op0=ALU.subtract, op1=ALU.mult)
                last.then_inc(dev_ok, 1)

            def v_sum(g, k, i):
                dve.wait_ge(dev_ok, g + 1)
                dve.wait_ge(rstd_ok[1], g + 1)
                dve.wait_ge(xb_ok, g + 1)
                reached(dve, fin_ok, g - 1)
                for t in range(T):
                    last = nc.vector.scalar_tensor_tensor(out=v[k][:, t, :], in0=dev[k][:, t, :], scalar=rstd[1][k][:, t:t + 1],
                                                          in1=x1_b2[k][:, t, :], op0=ALU.mult, op1=ALU.add)
                last.then_inc(v_ok, 1)
                dve.wait_ge(v_ok, g + 1)
                reached(dve, rstd_ok[2], g - 1)
                norm_stats(nc, dve, stat_c[2], g, v[k], stats[2][k], mom[2][k]).then_inc(mom_ok[2], 1)

            def turn(do):
                do(1, mean_shift(0, xh_ok))
                do(-1, residual)
                do(-2, v_sum)
                do(2, y_moments)
                do(-1, z_deviation)
                do(-2, mean_shift(2, fin_ok))
            turns(dve, turn)

        @block.tensor
        def _(pe):
            pe.wait_ge(wts, 8 * 16)

            def turn_y(g, k, i):
                pe.wait_ge(xh_ok, g + 1)
                reached(pe, h_ok, g)
                for t in range(T):
                    last = nc.tensor.transpose(bank[0][:, t * P:(t + 1) * P], xh[k][:, t, :], ident[:, :])
                last.then_inc(xh_t, 1)

            def turn_z(g, k, i):
                pe.wait_ge(z_ok, g + 1)
                reached(pe, dev_ok, g - 1)
                for t in range(T):
                    last = nc.tensor.transpose(z_bank[k][:, t * P:(t + 1) * P], z_c[k][:, t * P:(t + 1) * P], ident[:, :])
                last.then_inc(z_t, 1)

            def hidden(c):
                def step(g, k, i):
                    if c == 0:
                        pe.wait_ge(h_ok, g + 1)
                    reached(pe, ge, FC * g + 1 if c == 3 else FC * (g - 1) + (FC if c == 0 else c + 1))
                    nc.tensor.matmul(hid_bank[c][:, :], w1[:, c * P:(c + 1) * P], h_c[k][:, :], start=True, stop=True).then_inc(f1, 1)
                return step

            def output(c):
                def step(g, k, i):
                    pe.wait_ge(ge, FC * g + c + 1)
                    if c == 0:
                        reached(pe, z_ok, g - 1)
                    product = nc.tensor.matmul(out_bank[k][:, :], w2[:, c, :], act_c[c][:, :], start=(c == 0), stop=(c == FC - 1))
                    if c == FC - 1:
                        product.then_inc(f2, 1)
                return step

            def turn(do):
                do(0, hidden(0))
                do(0, hidden(1))
                do(0, hidden(2))
                do(1, turn_y)
                do(0, output(0))
                do(0, hidden(3))
                do(0, output(1))
                do(-1, turn_z)
                do(0, output(2))
                do(0, output(3))
            turns(pe, turn)

        @block.scalar
        def _(act):
            act.wait_ge(wts, 8 * 16)

            def h_cols(g, k, i):
                act.wait_ge(xh_t, g + 1)
                reached(act, z_ok, g - 1)
                nc.scalar.activation(h_c[k][:, :], bank[0][:, :], ACT.Identity, bias=b1[:, 0:1], scale=g1[:, 0:1]).then_inc(h_ok, 1)

            def gelu(c):
                def step(g, k, i):
                    act.wait_ge(f1, FC * g + c + 1)
                    if c == 0:
                        reached(act, f2, g)
                    nc.scalar.activation(act_c[c][:, :], hid_bank[c][:, :], ACT.Gelu, bias=bf1[:, c:c + 1]).then_inc(ge, 1)
                return step

            def normalize(m, src, dst, ready, g, k):
                act.wait_ge(shift_ok[m], g + 1)
                for t in range(T):
                    last = nc.scalar.activation(dst[:, t, :], src[:, t, :], ACT.Identity, bias=shift[m][k][:, t:t + 1],
                                                scale=rstd[m][k][:, t:t + 1])
                last.then_inc(ready, 1)

            def y_hat(g, k, i):
                reached(act, xh_t, g - 1)
                normalize(0, y[k], xh[k], xh_ok, g, k)

            def finish(g, k, i):
                reached(act, st[k], 16 * i)
                normalize(2, v[k], fin[k], fin_ok, g, k)

            def turn(do):
                do(1, y_hat)
                do(0, gelu(0))
                do(0, gelu(1))
                do(0, gelu(2))
                do(1, h_cols)
                do(0, gelu(3))
                do(-3, finish)
            turns(act, turn)


def build(nc, a, out):
    with ExitStack() as ctx:
        core = Core(nc, ctx)
        l1 = {name[7:]: ap for name, ap in a.items() if name.startswith("L1_gnn_")}
        make_identity(core)
        core.end_stage()
        sort_by_src(core, a["dst"], a["src"], a["x"], a["L0_gnn_W_edge"])
        core.end_stage()

        def by_src(sp, here, after, other, sem):
            return load_blocks(sp, here, core.by_src, NP, 0, sem) + load_blocks(sp, after, core.by_src, NP, 1, sem)

        def by_dst(sp, here, after, other, sem):
            return (load_blocks(sp, here, a["dst"], E, 0, sem) + load_blocks(sp, after, a["dst"], E, 1, sem)
                    + load_blocks(sp, other, a["src"], E, 0, sem))
        index_tables(core, "mpx_", by_src, True,
                     core.by_src.rearrange("(u e) w -> u e w", u=HALF)[:, 0, 0].rearrange("(a u) -> a u", a=1))
        core.end_stage()
        message_passing(core, a["x"], a["L0_gnn_W_edge"], a["L0_gnn_b_edge"], a["L0_gnn_W_agg"], a["L0_gnn_b_agg"])
        core.end_stage()
        index_tables(core, "atx_", by_dst, False)
        core.end_stage()
        project_nodes(core, a["x"], l1, l1)
        core.end_stage()
        attention(core, a["edge_attr_64"], l1["We"])
        core.end_stage()
        feed_forward(core, l1, out)


def kernel(**inputs):
    import numpy as np
    import concourse.bacc as bacc
    from concourse.bass_utils import run_bass_kernel_spmd as run

    nc = bacc.Bacc("TRN2", target_bir_lowering=False, num_devices=1)
    arrays, aps = {}, {}
    for name, value in inputs.items():
        value = np.ascontiguousarray(value)
        arrays["in_" + name] = value
        aps[name] = nc.dram_tensor("in_" + name, value.shape, mybir.dt.from_np(value.dtype), kind="ExternalInput").ap()
    out = nc.dram_tensor("out_rows", (N, D), F32, kind="ExternalOutput").ap()
    build(nc, aps, out)
    return run(nc, [arrays], core_ids=[0]).results[0]["out_rows"]
```
